# Optimizing a Trainium2 kernel written in Bass

```python
import numpy as np
import jax
import jax.numpy as jnp

def _softmax(x, axis=-1):
    return jax.nn.softmax(x, axis=axis)

def _gelu(x):
    return jax.nn.gelu(x, approximate=True)

def _silu(x):
    return jax.nn.silu(x)

def _sigmoid(x):
    return jax.nn.sigmoid(x)

def _layernorm(x, axis=-1, eps=1e-05):
    m = jnp.mean(x, axis=axis, keepdims=True)
    v = jnp.var(x, axis=axis, keepdims=True)
    return (x - m) / jnp.sqrt(v + eps)

def _scatter_add(tgt, idx, src, axis=0):
    return tgt.at[idx].add(src)

def _segment_sum(src, seg, n):
    return jax.ops.segment_sum(src, seg, n)
kernel_name = 'mk_conv_seq_d2_conv_nchw128_r2_345388'

def setup_inputs(seed: int=0):
    np.random.seed(seed)
    _w = jnp.asarray

    def _rec_inputs():
        import jax
        import jax.numpy as jnp
        _gk = jax.random.key(seed)
        x = -0.0003929 + 0.9999 * jax.random.normal(jax.random.fold_in(_gk, 1), (8, 64, 64, 64), jnp.float32)
        return x
    x = _rec_inputs()

    def _L0_conv_setup():
        import jax, jax.numpy as jnp
        import numpy as np
        import math
        C = 64
        H = 8
        HID = 2 * C
        MAX_LEN = 1000

        def _make_pe():
            pos = np.arange(MAX_LEN)[:, None].astype(np.float32)
            div = np.exp(np.arange(0, C, 2).astype(np.float32) * (-math.log(10000.0) / C))
            pe = np.zeros((MAX_LEN, C), dtype=np.float32)
            pe[:, 0::2] = np.sin(pos * div[None, :])
            pe[:, 1::2] = np.cos(pos * div[None, :])
            return jnp.asarray(pe)

        def _ln(x, g, b, eps=1e-05):
            mu = jnp.mean(x, -1, keepdims=True)
            var = jnp.var(x, -1, keepdims=True)
            return (x - mu) * jax.lax.rsqrt(var + eps) * g + b
        key = jax.random.key(seed)
        ks = jax.random.split(key, 24)
        s = 0.02
        d = {}
        d['x'] = jax.random.normal(ks[0], (8, C, 64, 64), jnp.float32)
        d['gn_g'] = jnp.ones((C,), jnp.float32)
        d['gn_b'] = jnp.zeros((C,), jnp.float32)
        d['ciw'] = jax.random.normal(ks[1], (C, C), jnp.float32) * s
        d['cib'] = jnp.zeros((C,), jnp.float32)
        d['pe'] = _make_pe()
        d['ln1g'] = jnp.ones((C,), jnp.float32)
        d['ln1b'] = jnp.zeros((C,), jnp.float32)
        d['wq'] = jax.random.normal(ks[2], (C, C), jnp.float32) * s
        d['bq'] = jnp.zeros((C,), jnp.float32)
        d['wk'] = jax.random.normal(ks[3], (C, C), jnp.float32) * s
        d['bk'] = jnp.zeros((C,), jnp.float32)
        d['wv'] = jax.random.normal(ks[4], (C, C), jnp.float32) * s
        d['bv'] = jnp.zeros((C,), jnp.float32)
        d['win'] = jax.random.normal(ks[5], (3 * C, C), jnp.float32) * s
        d['bin_'] = jnp.zeros((3 * C,), jnp.float32)
        d['wout'] = jax.random.normal(ks[6], (C, C), jnp.float32) * s
        d['bout'] = jnp.zeros((C,), jnp.float32)
        d['ln2g'] = jnp.ones((C,), jnp.float32)
        d['ln2b'] = jnp.zeros((C,), jnp.float32)
        d['w1'] = jax.random.normal(ks[7], (HID, C), jnp.float32) * s
        d['b1'] = jnp.zeros((HID,), jnp.float32)
        d['w2'] = jax.random.normal(ks[8], (HID, C), jnp.float32) * s
        d['b2'] = jnp.zeros((HID,), jnp.float32)
        d['w3'] = jax.random.normal(ks[9], (C, HID), jnp.float32) * s
        d['b3'] = jnp.zeros((C,), jnp.float32)
        d['cow'] = jax.random.normal(ks[10], (C, C), jnp.float32) * s
        d['cob'] = jnp.zeros((C,), jnp.float32)
        return d
    _L0_conv_all = _L0_conv_setup()
    _L0_conv_in = {k: v for k, v in _L0_conv_all.items() if k in ('gn_g', 'gn_b', 'ciw', 'cib', 'pe', 'ln1g', 'ln1b', 'wq', 'bq', 'wk', 'bk', 'wv', 'bv', 'win', 'bin_', 'wout', 'bout', 'ln2g', 'ln2b', 'w1', 'b1', 'w2', 'b2', 'w3', 'b3', 'cow', 'cob')}
    del _L0_conv_all

    def _L1_conv_setup():
        import jax, jax.numpy as jnp
        import numpy as np
        from jax import lax
        H_STEP = 1.0 / 3.0
        N_STEPS = 3

        def _conv(x, w):
            return lax.conv_general_dilated(x, w, window_strides=(1, 1), padding='SAME', dimension_numbers=('NCHW', 'OIHW', 'NCHW'))
        key = jax.random.key(seed)
        ks = jax.random.split(key, 5)
        B, C, H, W = (16, 64, 64, 64)
        fan_in = C * 9
        return {'x': jax.random.normal(ks[0], (B, C, H, W), dtype=jnp.float32), 'w1': jax.random.normal(ks[1], (C, C, 3, 3), dtype=jnp.float32) * (2.0 / fan_in) ** 0.5, 'b1': jax.random.normal(ks[2], (C,), dtype=jnp.float32) * 0.01, 'w2': jax.random.normal(ks[3], (C, C, 3, 3), dtype=jnp.float32) * (2.0 / fan_in) ** 0.5, 'b2': jax.random.normal(ks[4], (C,), dtype=jnp.float32) * 0.01}
    _L1_conv_all = _L1_conv_setup()
    _L1_conv_in = {k: v for k, v in _L1_conv_all.items() if k in ('w1', 'b1', 'w2', 'b2')}
    del _L1_conv_all
    return {'x': x, 'L0_conv_gn_g': _L0_conv_in['gn_g'], 'L0_conv_gn_b': _L0_conv_in['gn_b'], 'L0_conv_ciw': _L0_conv_in['ciw'], 'L0_conv_cib': _L0_conv_in['cib'], 'L0_conv_pe': _L0_conv_in['pe'], 'L0_conv_ln1g': _L0_conv_in['ln1g'], 'L0_conv_ln1b': _L0_conv_in['ln1b'], 'L0_conv_wq': _L0_conv_in['wq'], 'L0_conv_bq': _L0_conv_in['bq'], 'L0_conv_wk': _L0_conv_in['wk'], 'L0_conv_bk': _L0_conv_in['bk'], 'L0_conv_wv': _L0_conv_in['wv'], 'L0_conv_bv': _L0_conv_in['bv'], 'L0_conv_win': _L0_conv_in['win'], 'L0_conv_bin_': _L0_conv_in['bin_'], 'L0_conv_wout': _L0_conv_in['wout'], 'L0_conv_bout': _L0_conv_in['bout'], 'L0_conv_ln2g': _L0_conv_in['ln2g'], 'L0_conv_ln2b': _L0_conv_in['ln2b'], 'L0_conv_w1': _L0_conv_in['w1'], 'L0_conv_b1': _L0_conv_in['b1'], 'L0_conv_w2': _L0_conv_in['w2'], 'L0_conv_b2': _L0_conv_in['b2'], 'L0_conv_w3': _L0_conv_in['w3'], 'L0_conv_b3': _L0_conv_in['b3'], 'L0_conv_cow': _L0_conv_in['cow'], 'L0_conv_cob': _L0_conv_in['cob'], 'L1_conv_w1': _L1_conv_in['w1'], 'L1_conv_b1': _L1_conv_in['b1'], 'L1_conv_w2': _L1_conv_in['w2'], 'L1_conv_b2': _L1_conv_in['b2']}

def reference(x, L0_conv_gn_g, L0_conv_gn_b, L0_conv_ciw, L0_conv_cib, L0_conv_pe, L0_conv_ln1g, L0_conv_ln1b, L0_conv_wq, L0_conv_bq, L0_conv_wk, L0_conv_bk, L0_conv_wv, L0_conv_bv, L0_conv_win, L0_conv_bin_, L0_conv_wout, L0_conv_bout, L0_conv_ln2g, L0_conv_ln2b, L0_conv_w1, L0_conv_b1, L0_conv_w2, L0_conv_b2, L0_conv_w3, L0_conv_b3, L0_conv_cow, L0_conv_cob, L1_conv_w1, L1_conv_b1, L1_conv_w2, L1_conv_b2):
    import jax
    import jax.numpy as jnp

    def _L0_conv_ref(x, gn_g, gn_b, ciw, cib, pe, ln1g, ln1b, wq, bq, wk, bk, wv, bv, win, bin_, wout, bout, ln2g, ln2b, w1, b1, w2, b2, w3, b3, cow, cob):
        import jax, jax.numpy as jnp
        import numpy as np
        import math
        C = 64
        H = 8
        HID = 2 * C
        MAX_LEN = 1000

        def _make_pe():
            pos = np.arange(MAX_LEN)[:, None].astype(np.float32)
            div = np.exp(np.arange(0, C, 2).astype(np.float32) * (-math.log(10000.0) / C))
            pe = np.zeros((MAX_LEN, C), dtype=np.float32)
            pe[:, 0::2] = np.sin(pos * div[None, :])
            pe[:, 1::2] = np.cos(pos * div[None, :])
            return jnp.asarray(pe)

        def _ln(x, g, b, eps=1e-05):
            mu = jnp.mean(x, -1, keepdims=True)
            var = jnp.var(x, -1, keepdims=True)
            return (x - mu) * jax.lax.rsqrt(var + eps) * g + b
        b, c, h, w = x.shape
        hd = c // H
        res_long = x
        xg = x.reshape(b, 8, c // 8, h, w)
        mu = jnp.mean(xg, (2, 3, 4), keepdims=True)
        var = jnp.var(xg, (2, 3, 4), keepdims=True)
        xn = ((xg - mu) * jax.lax.rsqrt(var + 1e-06)).reshape(b, c, h, w)
        xn = xn * gn_g[None, :, None, None] + gn_b[None, :, None, None]
        xc = jnp.einsum('bchw,oc->bohw', xn, ciw) + cib[None, :, None, None]
        t = xc.reshape(b, c, h * w).transpose(0, 2, 1)
        t = t + pe[:b][:, None, :]
        tn = _ln(t, ln1g, ln1b)
        q = tn @ wq.T + bq
        k = tn @ wk.T + bk
        v = tn @ wv.T + bv
        wiq, wik, wiv = jnp.split(win, 3, axis=0)
        biq, bik, biv = jnp.split(bin_, 3, axis=0)
        q2 = (q @ wiq.T + biq).reshape(b, h * w, H, hd)
        k2 = (k @ wik.T + bik).reshape(b, h * w, H, hd)
        v2 = (v @ wiv.T + biv).reshape(b, h * w, H, hd)
        scores = jnp.einsum('inhd,jnhd->nhij', q2, k2) / jnp.sqrt(jnp.float32(hd))
        attn = jax.nn.softmax(scores, axis=-1)
        z = jnp.einsum('nhij,jnhd->inhd', attn, v2).reshape(b, h * w, c)
        z = z @ wout.T + bout
        t = z + t
        tn2 = _ln(t, ln2g, ln2b)
        a = tn2 @ w1.T + b1
        g = t @ w2.T + b2
        m = a * jax.nn.gelu(g, approximate=False) @ w3.T + b3
        t = m + t
        y = t.transpose(0, 2, 1).reshape(b, c, h, w)
        out = jnp.einsum('bchw,oc->bohw', y, cow) + cob[None, :, None, None] + res_long
        return out

    def _L1_conv_ref(x, w1, b1, w2, b2):
        import jax, jax.numpy as jnp
        import numpy as np
        from jax import lax
        H_STEP = 1.0 / 3.0
        N_STEPS = 3

        def _conv(x, w):
            return lax.conv_general_dilated(x, w, window_strides=(1, 1), padding='SAME', dimension_numbers=('NCHW', 'OIHW', 'NCHW'))
        for _ in range(N_STEPS):
            t = jax.nn.relu(_conv(x, w1) + b1[None, :, None, None])
            x = x + H_STEP * (_conv(t, w2) + b2[None, :, None, None])
        return jax.nn.relu(x)

    def _gn(v, G=32, eps=1e-05):
        B_, C_, H_, W_ = v.shape
        g = v.reshape(B_, G, C_ // G, H_, W_)
        m = jnp.mean(g, axis=(2, 3, 4), keepdims=True)
        s = jnp.var(g, axis=(2, 3, 4), keepdims=True)
        return ((g - m) / jnp.sqrt(s + eps)).reshape(v.shape)

    def _ln_c(v, eps=1e-06):
        m = jnp.mean(v, axis=1, keepdims=True)
        s = jnp.var(v, axis=1, keepdims=True)
        return (v - m) / jnp.sqrt(s + eps)

    def _ln_t(v, eps=1e-05):
        m = jnp.mean(v, axis=-1, keepdims=True)
        s = jnp.var(v, axis=-1, keepdims=True)
        return (v - m) / jnp.sqrt(s + eps)

    def _to_tokens(v):
        B_, C_, H_, W_ = v.shape
        return v.reshape(B_, C_, H_ * W_).transpose(0, 2, 1)

    def _from_tokens(t, like):
        B_, C_, H_, W_ = like.shape
        return t.transpose(0, 2, 1).reshape(B_, C_, H_, W_)
    x = _L0_conv_ref(x, L0_conv_gn_g, L0_conv_gn_b, L0_conv_ciw, L0_conv_cib, L0_conv_pe, L0_conv_ln1g, L0_conv_ln1b, L0_conv_wq, L0_conv_bq, L0_conv_wk, L0_conv_bk, L0_conv_wv, L0_conv_bv, L0_conv_win, L0_conv_bin_, L0_conv_wout, L0_conv_bout, L0_conv_ln2g, L0_conv_ln2b, L0_conv_w1, L0_conv_b1, L0_conv_w2, L0_conv_b2, L0_conv_w3, L0_conv_b3, L0_conv_cow, L0_conv_cob)
    x = _L1_conv_ref(x, L1_conv_w1, L1_conv_b1, L1_conv_w2, L1_conv_b2)
    return x

_drawn_inputs = setup_inputs


def setup_inputs(seed=0):
    import zlib

    import numpy as np

    out = dict(_drawn_inputs(seed))
    spreads = {'L0_conv_gn_g': (1.0, 0.6),
     'L0_conv_gn_b': (0.0, 0.8),
     'L0_conv_cib': (0.0, 0.667),
     'L0_conv_ln1g': (1.0, 0.6),
     'L0_conv_ln1b': (0.0, 0.8),
     'L0_conv_bq': (0.0, 0.8),
     'L0_conv_bk': (0.0, 2.0),
     'L0_conv_bv': (0.0, 0.8),
     'L0_conv_bin_': (0.0, 0.8),
     'L0_conv_bout': (0.0, 0.532),
     'L0_conv_ln2g': (1.0, 0.6),
     'L0_conv_ln2b': (0.0, 0.8),
     'L0_conv_b1': (0.0, 0.8),
     'L0_conv_b2': (0.0, 0.8),
     'L0_conv_b3': (0.0, 0.471),
     'L0_conv_cob': (0.0, 0.1)}
    factors = {'L0_conv_wq': 8.0,
     'L0_conv_wk': 8.0,
     'L0_conv_wv': 8.0,
     'L0_conv_win': 8.0,
     'L0_conv_wout': 8.0,
     'L0_conv_w1': 8.0,
     'L0_conv_w2': 8.0,
     'L0_conv_w3': 8.0,
     'L1_conv_b1': 26.513,
     'L1_conv_b2': 25.915}
    for name, (base, spread) in spreads.items():
        noise = np.random.default_rng([zlib.crc32(name.encode()), seed]).standard_normal(out[name].shape)
        drawn = base * np.exp(spread * noise) if base else spread * noise
        out[name] = jnp.asarray(drawn.astype(out[name].dtype))
    for name, factor in factors.items():
        out[name] = (out[name] * factor).astype(out[name].dtype)
    return out
```

```python
import concourse.bass as bass
from concourse import mybir
from contextlib import ExitStack

B, C, HW = 8, 64, 64
HEADS = 8
HD = C // HEADS
HID = 2 * C
PIX = HW * HW
TILE = 2 * HW
TILES = PIX // TILE
PAIRS = B // 2
P = 2 * C
SLOTS = HW // 2 + 1
PADW = HW + 2
STEPS = 3
H_STEP = 1.0 / 3.0
TAPS = 3
POOL_I = 3
F32, F32R = mybir.dt.float32, mybir.dt.float32r
ALU, ACT, AX = mybir.AluOpType, mybir.ActivationFunctionType, mybir.AxisListType
K_ID, K_CEN, K_GRP, K_MEAN, K_END = 0, P, 2 * P, 3 * P, 3 * P + 2


def wait(eng, sem, n):
    if isinstance(n, int) and n <= 0:
        return
    eng.wait_ge(sem, n)


def setup_weights(nc, d, s, top):
    with ExitStack() as ctx:
        def sb(name, shape, dt=F32):
            return ctx.enter_context(nc.sbuf_tensor(name, shape, dt))

        def ps(name, shape):
            return ctx.enter_context(nc.psum_tensor(name, shape, F32))

        def sem(name):
            return ctx.enter_context(nc.semaphore(name))

        win = sb("win", [C, 3, C])
        wqkv = sb("wqkv", [C, 3, C])
        ciw = sb("ciw", [C, C])
        wout2 = sb("wout2", [C, 2, C])
        cow2 = sb("cow2", [C, 2, C])
        w1n = sb("w1n", [HID, 2, C])
        w2n = sb("w2n", [HID, 2, C])
        w3n = sb("w3n", [C, HID])
        binr = sb("binr", [1, 3 * C])
        ones1 = sb("ones1", [1, P])
        vec = sb("vec", [C, 12])
        pen = sb("pen", [B, C])
        pet = sb("pet", [C, B])
        cw = [sb(f"cw{k}", [C, C, TAPS * TAPS]) for k in range(2)]
        cw2 = sb("cw2", [C, TAPS * TAPS, 2, C])
        wiT = sb("wiT", [C, 3, C])
        rq = sb("rq", [C, 3 * C])
        rqg = sb("rqg", [C, 3 * C])
        basis = sb("basis", [C, 4 * C])
        reps = sb("reps", [C, 4, P])
        w1raw = sb("w1raw", [P, HID])
        wall = sb("wall", [C, 4 * C])
        cowrep = sb("cowrep", [C, 2, C])
        convf = sb("convf", [P, 2, TAPS, P])
        xst = [sb(f"xst{k}", [P, PIX]) for k in range(2)]
        st = sb("st", [P, 8, 6])
        mv = sb("mv", [P, PAIRS, 2])
        means = sb("means", [P, PAIRS])
        dev = sb("dev", [P, PAIRS])
        wvar = sb("wvar", [P, PAIRS])
        mu = sb("mu", [C, B])
        gvar = sb("gvar", [C, B])
        gexp = sb("gexp", [C, B])
        ga = sb("ga", [C, B])
        gb = sb("gb", [C, B])
        cvec = sb("cvec", [C, B])
        beta = sb("beta", [B, 4 * C])
        pt = [ps(f"pset{k}", [P, 512]) for k in range(8)]

        loaded, xin, pe_done, dve_done = sem("loaded"), [sem("xin0"), sem("xin1")], sem("pe_done"), sem("dve_done")
        rs_ready, beta_moved = sem("rs_ready"), sem("beta_moved")
        GN_G, GN_B, LN1G, LN1B, BQ, BK, BV, CIB, B3, LN2B = range(10)
        ident, center = top["consts"][:, K_ID:K_ID + P], top["consts"][:, K_CEN:K_CEN + P]
        group = top["consts"][:, K_GRP:K_GRP + P]

        loads = [
            (top["consts"][:, :], d["consts"]),
            (win[:, :, :], d["L0_conv_win"].rearrange("(t o) i -> o t i", t=3)),
            (wqkv[:, 0, :], d["L0_conv_wq"]), (wqkv[:, 1, :], d["L0_conv_wk"]), (wqkv[:, 2, :], d["L0_conv_wv"]),
            (ciw[:, :], d["L0_conv_ciw"]), (w3n[:, :], d["L0_conv_w3"]),
            (binr[:, :], d["L0_conv_bin_"].rearrange("(a n) -> a n", a=1)),
            (pen[:, :], d["L0_conv_pe"][0:B, :]),
        ]
        for k in range(2):
            loads += [(wout2[:, k, :], d["L0_conv_wout"]), (cow2[:, k, :], d["L0_conv_cow"]),
                      (w1n[:, k, :], d["L0_conv_w1"]), (w2n[:, k, :], d["L0_conv_w2"]),
                      (cw[k][:, :, :], d[f"L1_conv_w{k + 1}"].rearrange("o i a b -> o i (a b)"))]
            half = slice(C * k, C * k + C)
            for col, name in ((0, "L0_conv_ln2g"), (1, "L0_conv_bout"), (4, "L0_conv_cob"),
                              (6, "L1_conv_b1"), (7, "L1_conv_b2")):
                loads.append((top["cols"][half, col:col + 1], d[name].rearrange("(n a) -> n a", a=1)))
        for col, name in ((2, "L0_conv_b1"), (3, "L0_conv_b2")):
            loads.append((top["cols"][:, col:col + 1], d[name].rearrange("(n a) -> n a", a=1)))
        for col, name in ((GN_G, "L0_conv_gn_g"), (GN_B, "L0_conv_gn_b"), (LN1G, "L0_conv_ln1g"),
                          (LN1B, "L0_conv_ln1b"), (BQ, "L0_conv_bq"), (BK, "L0_conv_bk"), (BV, "L0_conv_bv"),
                          (CIB, "L0_conv_cib"), (B3, "L0_conv_b3"), (LN2B, "L0_conv_ln2b")):
            loads.append((vec[:, col:col + 1], d[name].rearrange("(n a) -> n a", a=1)))
        all_loaded = 16 * len(loads)
        at = {}

        block = ctx.enter_context(nc.Block())

        def x_pair(p):
            return d["x"][2 * p:2 * p + 2].rearrange("b c h w -> (b c) (h w)")

        @block.vector
        def _(dve):
            n = [0]

            def link(ins, name=None):
                n[0] += 1
                ins.then_inc(dve_done, 1)
                dve.wait_ge(dve_done, n[0])
                if name:
                    at[name] = n[0]

            link(dve.memset(ones1[:, :], 1.0))
            link(dve.memset(gexp[:, :], -0.5))
            link(dve.memset(top["half"][:, :], -0.5))
            for k in range(2):
                link(dve.memset(top["xt"][k][C:C + 1, :, :], 1.0))
            link(dve.memset(top["woutT"][:, :], 0.0), "zeros")
            dve.wait_ge(loaded, all_loaded)
            for k, col in enumerate((LN1B, BQ, BK, BV)):
                link(dve.tensor_copy(reps[:, k, :], vec[:, col:col + 1].broadcast_to([C, P])))
            dve.wait_ge(pe_done, 1)
            link(dve.tensor_copy(wiT[:, :, :], pt[0][0:C, 0:3 * C].rearrange("p (t o) -> p t o", t=3)), "wiT")
            dve.wait_ge(pe_done, 2)
            for k in range(2):
                half = slice(C * k, C * k + C)
                link(dve.tensor_copy(top["woutT"][half, half], pt[1][half, 0:C]))
            link(dve.tensor_copy(pet[:, :], pt[1][0:C, 2 * C:2 * C + B]))
            link(dve.tensor_copy(top["cowT"][:, :], pt[1][:, C:2 * C]))
            for k in range(2):
                link(dve.tensor_copy(cowrep[:, k, :], pt[1][0:C, C:2 * C]), "cowT")
            dve.wait_ge(pe_done, 3)
            link(dve.tensor_copy(w1raw[:, :], pt[2][:, 0:HID]))
            link(dve.tensor_scalar(top["w1T"][:, :], pt[2][:, 0:HID], top["cols"][:, 0:1], None, ALU.mult))
            link(dve.tensor_copy(top["w2T"][:, :], pt[2][:, HID:2 * HID]), "w1raw")
            dve.wait_ge(pe_done, 4)
            link(dve.tensor_copy(rq[:, :], pt[3][0:C, 0:3 * C]))
            link(dve.tensor_scalar(rqg[:, :], pt[3][0:C, 0:3 * C], vec[:, LN1G:LN1G + 1], None, ALU.mult), "rq")
            dve.wait_ge(pe_done, 6)
            link(dve.tensor_copy(basis[:, 0:C], ident[0:C, 0:C]))
            for k in range(2):
                cols = slice(C * (k + 1), C * (k + 2))
                link(dve.tensor_copy(basis[:, cols].rearrange("p (e h) -> p e h", h=HEADS),
                                     pt[4][0:C, C * k:C * (k + 1)].rearrange("p (h e) -> p e h", h=HEADS)))
                link(dve.tensor_copy(top["brep"][:, C * k:C * (k + 1)].rearrange("p (e h) -> p e h", h=HEADS),
                                     pt[5][:, C * k:C * (k + 1)].rearrange("p (h e) -> p e h", h=HEADS)))
            link(dve.tensor_copy(basis[:, 3 * C:4 * C], pt[4][0:C, 2 * C:3 * C]))
            link(dve.tensor_copy(top["brep"][:, 2 * C:3 * C], pt[5][:, 2 * C:3 * C]), "basis")
            dve.wait_ge(pe_done, 7)
            link(dve.tensor_copy(wall[:, :], pt[0][0:C, 0:4 * C]), "wall")
            dve.wait_ge(pe_done, 8)
            link(dve.tensor_copy(top["w3T"][:, :], pt[1][:, 0:C]))
            dve.wait_ge(pe_done, 9)
            link(dve.tensor_tensor(top["cols"][:, 4:5], pt[2][:, 0:1], top["cols"][:, 4:5], ALU.add))
            link(dve.tensor_tensor(top["cols"][:, 2:3], pt[2][:, 8:9], top["cols"][:, 2:3], ALU.add))
            link(dve.tensor_scalar(top["cols"][:, 8:9], top["cols"][:, 7:8], H_STEP, None, ALU.mult), "small")
            for k in range(2):
                link(dve.tensor_copy(cw2[:, :, 0, :], cw[k][:, :, :].rearrange("o i t -> o t i")))
                link(dve.tensor_copy(cw2[:, :, 1, :], cw[k][:, :, :].rearrange("o i t -> o t i")), f"cw{k}")
                link(dve.memset(convf[:, :, :, :], 0.0))
                dve.wait_ge(pe_done, 10 + k)
                for ky in range(TAPS):
                    for a in range(2):
                        for b in range(2):
                            for slot in range(2):
                                if 2 * slot + a - b == ky:
                                    ra, rb = slice(C * a, C * a + C), slice(C * b, C * b + C)
                                    link(dve.tensor_copy(
                                        convf[ra, slot, :, rb],
                                        pt[3 + ky][ra, 0:TAPS * C].rearrange("p (t o) -> p t o", t=TAPS)), f"cwout{k}")
                link(dve.tensor_copy(top["cwh"][k][:, :, :, :], convf[:, :, :, :]))
                link(dve.tensor_tensor(top["cwl"][k][:, :, :, :], convf[:, :, :, :],
                                       top["cwh"][k][:, :, :, :].bitcast(F32), ALU.subtract))
            for p in range(PAIRS):
                dve.wait_ge(xin[p % 2], 16 * (p // 2 + 1))
                for q in range(8):
                    link(dve.bn_stats(st[:, q, :], xst[p % 2][:, 512 * q:512 * (q + 1)]), f"x{p}")
                link(dve.bn_aggr(mv[:, p, :], st[:, :, :]))
            link(dve.tensor_copy(means[:, :], mv[:, :, 0]), "means")
            dve.wait_ge(pe_done, 12)
            link(dve.tensor_tensor(dev[:, :], means[:, :], pt[6][:, 0:PAIRS], ALU.subtract))
            link(dve.tensor_tensor(dev[:, :], dev[:, :], dev[:, :], ALU.mult))
            link(dve.tensor_tensor(wvar[:, :], mv[:, :, 1], dev[:, :], ALU.add), "wvar")
            dve.wait_ge(pe_done, 13)
            link(dve.tensor_copy(mu[:, :].rearrange("c (p e) -> c e p", e=2),
                                 pt[7][0:C, 0:B].rearrange("c (e p) -> c e p", e=2)))
            link(dve.tensor_scalar(gvar[:, :].rearrange("c (p e) -> c e p", e=2),
                                   pt[7][0:C, B:2 * B].rearrange("c (e p) -> c e p", e=2), 1e-6, None, ALU.add), "gvar")
            dve.wait_ge(rs_ready, 1)
            link(dve.tensor_scalar(ga[:, :], ga[:, :], vec[:, GN_G:GN_G + 1], None, ALU.mult))
            link(dve.tensor_tensor(mu[:, :], mu[:, :], ga[:, :], ALU.mult))
            link(dve.tensor_scalar(gb[:, :], mu[:, :], -1.0, vec[:, GN_B:GN_B + 1], ALU.mult, ALU.add), "gb")
            for i in range(B):
                link(dve.tensor_scalar(top["wcat"][0:C, i, :], wall[:, :], ga[:, i:i + 1], None, ALU.mult))
            dve.wait_ge(pe_done, 14)
            link(dve.scalar_tensor_tensor(cvec[:, :], pt[0][0:C, 0:B], vec[:, CIB:CIB + 1], pet[:, :],
                                          ALU.add, ALU.add), "cvec")
            dve.wait_ge(pe_done, 15)
            link(dve.tensor_copy(beta[:, :], pt[1][0:B, 0:4 * C]), "beta")

        @block.sync
        def _(sp):
            for k, (dst, src) in enumerate(loads):
                if k % 2 == 0:
                    sp.dma_start(dst, src).then_inc(loaded, 16)
            for p in range(PAIRS):
                if p >= 2:
                    sp.wait_ge(dve_done, at[f"x{p - 2}"])
                sp.dma_start(xst[p % 2][:, :], x_pair(p)).then_inc(xin[p % 2], 16)
            sp.wait_ge(dve_done, at["beta"])
            sp.dma_start(top["wcat"][C:C + 1, :, :], beta[:, :]).then_inc(beta_moved, 16)
            sp.wait_ge(beta_moved, 16)

        @block.scalar
        def _(act):
            for k, (dst, src) in enumerate(loads):
                if k % 2 == 1:
                    act.dma_start(dst, src).then_inc(loaded, 16)

        @block.gpsimd
        def _(pool):
            pool.wait_ge(dve_done, at["gvar"])
            pool.tensor_tensor(ga[:, :], gvar[:, :], gexp[:, :], ALU.pow).then_inc(rs_ready, 1)

        @block.tensor
        def _(pe):
            def need(name):
                pe.wait_ge(dve_done, at[name])

            pe.wait_ge(loaded, all_loaded)
            for t in range(3):
                m = pe.transpose(pt[0][0:C, C * t:C * (t + 1)], win[:, t, :], ident[0:C, 0:C])
            m.then_inc(pe_done, 1)
            pe.transpose(pt[1][:, 0:C], wout2[:, :, :].rearrange("p a b -> p (a b)"), ident[0:C, 0:C])
            pe.transpose(pt[1][0:C, 2 * C:2 * C + B], pen[:, :], ident[0:B, 0:B])
            pe.transpose(pt[1][:, C:2 * C], cow2[:, :, :].rearrange("p a b -> p (a b)"),
                         ident[0:C, 0:C]).then_inc(pe_done, 1)
            pe.transpose(pt[2][:, 0:HID], w1n[:, :, :].rearrange("p a b -> p (a b)"), ident)
            pe.transpose(pt[2][:, HID:2 * HID], w2n[:, :, :].rearrange("p a b -> p (a b)"),
                         ident).then_inc(pe_done, 1)
            need("wiT")
            for t in range(3):
                m = pe.matmul(pt[3][0:C, C * t:C * (t + 1)], wqkv[:, t, :], wiT[:, t, :], start=True, stop=True)
            m.then_inc(pe_done, 1)
            need("rq")
            pe.matmul(pt[4][0:C, 0:3 * C], center[0:C, 0:C], rqg[:, :], start=True, stop=True).then_inc(pe_done, 1)
            pe.matmul(pt[5][:, 0:3 * C], reps[:, 0, :], rq[:, :], start=True, stop=False)
            for t in range(3):
                pe.matmul(pt[5][:, C * t:C * (t + 1)], reps[:, 1 + t, :], wiT[:, t, :], start=False, stop=False)
            pe.matmul(pt[5][:, 0:3 * C], ones1[:, :], binr[:, :], start=False, stop=True).then_inc(pe_done, 1)
            need("basis")
            pe.matmul(pt[0][0:C, 0:4 * C], ciw[:, :], basis[:, :], start=True, stop=True).then_inc(pe_done, 1)
            need("cowT")
            pe.matmul(pt[1][:, 0:C], w3n[:, :], top["cowT"][0:C, :], start=True, stop=True).then_inc(pe_done, 1)
            need("w1raw")
            pe.matmul(pt[2][:, 0:1], cowrep[:, :, :].rearrange("p a b -> p (a b)"), vec[:, B3:B3 + 1],
                      start=True, stop=True)
            pe.matmul(pt[2][:, 8:9], w1raw[0:C, :], vec[:, LN2B:LN2B + 1], start=True, stop=True)\
                .then_inc(pe_done, 1)
            for k in range(2):
                need(f"cw{k}")
                if k:
                    need("cwout0")
                for ky in range(TAPS):
                    for kx in range(TAPS):
                        m = pe.transpose(pt[3 + ky][:, C * kx:C * (kx + 1)],
                                         cw2[:, TAPS * ky + kx, :, :].rearrange("p a b -> p (a b)"), ident[0:C, 0:C])
                m.then_inc(pe_done, 1)
            need("means")
            pe.matmul(pt[6][:, 0:PAIRS], group, means[:, :], start=True, stop=True).then_inc(pe_done, 1)
            need("wvar")
            for k, src in enumerate((means, wvar)):
                for e in range(2):
                    m = pe.matmul(pt[7][0:C, B * k + PAIRS * e:B * k + PAIRS * (e + 1)], group[:, C * e:C * (e + 1)],
                                  src[:, :], start=True, stop=True)
            m.then_inc(pe_done, 1)
            need("gb")
            pe.matmul(pt[0][0:C, 0:B], wall[:, 0:C], gb[:, :], start=True, stop=True).then_inc(pe_done, 1)
            need("cvec")
            pe.matmul(pt[1][0:B, 0:4 * C], cvec[:, :], basis[:, :], start=True, stop=True).then_inc(pe_done, 1)


def attention_block(nc, d, top):
    with ExitStack() as ctx:
        def sb(name, shape, dt=F32):
            return ctx.enter_context(nc.sbuf_tensor(name, shape, dt))

        def ps(name, shape):
            return ctx.enter_context(nc.psum_tensor(name, shape, F32))

        def sem(name):
            return ctx.enter_context(nc.semaphore(name))

        N = PAIRS * TILE
        S = B * B * HEADS
        raw = [sb(f"raw{k}", [P, B, 4 * C]) for k in range(2)]
        qkv = [sb(f"qkv{k}", [P, B, 3 * C]) for k in range(2)]
        xr = [sb(f"xr{k}", [P, B, HW]) for k in range(2)]
        prod1 = sb("prod1", [P, HD, S])
        prod2 = sb("prod2", [P, B, B * C])
        st1 = sb("st1", [P, B, 6])
        tiny = sb("tiny", [P, 4, B])
        rstd1 = sb("rstd1", [P, B])
        rstd2 = sb("rstd2", [P, B])
        var2 = sb("var2", [P, B])
        scoresT = sb("scoresT", [P, 4, P])
        smax = sb("smax", [P, C])
        shifted = sb("shifted", [P, S])
        exps = sb("exps", [P, S])
        den = sb("den", [P, C])
        rden = sb("rden", [P, C])
        attn = sb("attn", [P, S])
        z = sb("z", [P, N])
        z1 = sb("z1", [P, N])
        cen2 = sb("cen2", [P, N])
        sq2 = sb("sq2", [P, N])
        tn2 = sb("tn2", [P, N])
        gel = [sb(f"gel{e}", [P, N]) for e in range(2)]
        gated = [sb(f"gated{e}", [P, N]) for e in range(2)]

        q_ps = [ps(f"q_ps{k}", [P, 2, 4 * C]) for k in range(2)]
        b2 = ps("b2", [P, 512])
        b3 = ps("b3", [P, 512])
        b4 = ps("b4", [P, 512])
        b5 = ps("b5", [P, 512])
        b6 = ps("b6", [P, 512])
        b7 = ps("b7", [P, 512])

        xt_in = [sem("xt_in0"), sem("xt_in1")]
        xr_in = [sem("xr_in0"), sem("xr_in1")]
        qkv_mm, scoresT_mm, scores_mm, av_mm = sem("qkv_mm"), sem("scoresT_mm"), sem("scores_mm"), sem("av_mm")
        z1_mm, cen2_mm, g_mm, var2_mm = sem("z1_mm"), sem("cen2_mm"), sem("g_mm"), sem("var2_mm")
        rstd2_mm, a_mm, out_mm = sem("rstd2_mm"), sem("a_mm"), sem("out_mm")
        raw_out, scoresT_out, z_out, z1_out = sem("raw_out"), sem("scoresT_out"), sem("z_out"), sem("z1_out")
        sq2_out, cen2_out, exp_out, gelu_out = sem("sq2_out"), sem("cen2_out"), sem("exp_out"), sem("gelu_out")
        stats_done, tiny_done, smax_done, shift_done = sem("stats_done"), sem("tiny_done"), sem("smax_done"), sem("shift_done")
        den_done, rden_done, qkv_done, p1_dve = sem("den_done"), sem("rden_done"), sem("qkv_done"), sem("p1_dve")
        p2_dve, tn2_done, gated_done, x_done = sem("p2_dve"), sem("tn2_done"), sem("gated_done"), sem("x_done")
        var2_done = sem("var2_done")
        rstd1_done, rstd2_done, attn_done = sem("rstd1_done"), sem("rstd2_done"), sem("attn_done")
        p1_pool, p2_pool = sem("p1_pool"), sem("p2_pool")

        ident, center = top["consts"][:, K_ID:K_ID + P], top["consts"][:, K_CEN:K_CEN + P]
        cmean = top["consts"][:, K_MEAN:K_MEAN + 2]
        cols = top["cols"]
        ND, NP = B - POOL_I, POOL_I
        x_flat = d["x"].rearrange("b c h w -> c b (h w)")
        x_rows = d["x"].rearrange("b c h w -> c b h w")
        xs = top["xs"]

        def p1_product(eng, k, i):
            v = qkv[k]
            q = v[:, i, 0:C].rearrange("p (e h) -> p e h", h=HEADS).unsqueeze(2).broadcast_to([P, HD, B, HEADS])
            kk = v[:, :, C:2 * C].rearrange("p j (e h) -> p e j h", h=HEADS)
            out = prod1[:, :, C * i:C * (i + 1)].rearrange("p e (j h) -> p e j h", h=HEADS)
            return eng.tensor_tensor(out, q, kk, ALU.mult)

        def p2_product(eng, k, j):
            a = attn[:, :].rearrange("p (i j h) -> p j i h", i=B, j=B)[:, j].unsqueeze(3).broadcast_to([P, B, HEADS, HD])
            v = qkv[k][:, j, 2 * C:3 * C].rearrange("p (h e) -> p h e", h=HEADS).unsqueeze(1).broadcast_to([P, B, HEADS, HD])
            out = prod2[:, j, :].rearrange("p (i h e) -> p i h e", i=B, h=HEADS)
            return eng.tensor_tensor(out, a, v, ALU.mult)

        def pe_qkv(pe, t, k, g):
            if g == 0:
                pe.wait_ge(xt_in[k], 16 * ((t - k) // 2 + 1) if isinstance(t, int) else (t - k) * 8 + 16)
            wait(pe, raw_out, 4 * t + g - 1)
            for e in range(2):
                m = pe.matmul(q_ps[g % 2][:, e, :], top["xt"][k][:, 2 * g + e, :], top["wcat"][:, 2 * g + e, :],
                              start=True, stop=True)
            m.then_inc(qkv_mm, 1)

        def pe_scores_t(pe, t):
            wait(pe, p1_dve, ND * (t + 1))
            wait(pe, p1_pool, NP * (t + 1))
            wait(pe, tn2_done, t - 1)
            for blk in range(4):
                for e in range(HD):
                    m = pe.matmul(b2[:, P * blk:P * (blk + 1)], prod1[:, e, P * blk:P * (blk + 1)], ident,
                                  start=(e == 0), stop=(e == HD - 1), is_transpose=True)
            m.then_inc(scoresT_mm, 1)

        def pe_scores(pe, t):
            wait(pe, scoresT_out, t + 1)
            wait(pe, shift_done, t)
            for blk in range(4):
                m = pe.transpose(b3[:, P * blk:P * (blk + 1)], scoresT[:, blk, :], ident)
            m.then_inc(scores_mm, 1)

        def pe_av(pe, t):
            wait(pe, p2_dve, ND * (t + 1))
            wait(pe, p2_pool, NP * (t + 1))
            wait(pe, gated_done, 2 * t - 1)
            for p in range(PAIRS):
                for j in range(B):
                    m = pe.matmul(b4[:, TILE * p:TILE * (p + 1)], prod2[:, j, P * p:P * (p + 1)], ident,
                                  start=(j == 0), stop=(j == B - 1), is_transpose=True)
            m.then_inc(av_mm, 1)

        def pe_z1(pe, t, k):
            wait(pe, z_out, t + 1)
            wait(pe, x_done, 4 * t)
            pe.matmul(b5[:, :], top["woutT"][:, :], z[:, :], start=True, stop=False)
            for p in range(PAIRS):
                m = pe.matmul(b5[:, TILE * p:TILE * (p + 1)], traw[k][:, 2 * p:2 * p + 2, :], ident,
                              start=False, stop=(p == PAIRS - 1), is_transpose=True)
            m.then_inc(z1_mm, 1)

        traw = [sb(f"traw{k}", [P, B, C]) for k in range(2)]

        def pe_center(pe, t):
            wait(pe, z1_out, t + 1)
            pe.matmul(b4[:, :], center, z1[:, :], start=True, stop=True).then_inc(cen2_mm, 1)

        def pe_g(pe, t, e):
            if e == 0:
                wait(pe, gated_done, 2 * t)
            half = slice(C * e, C * e + C)
            pe.matmul((b6, b7)[e][:, :], top["w2T"][half, :], z1[half, :], start=True, stop=True).then_inc(g_mm, 1)

        def pe_var2(pe, t):
            wait(pe, sq2_out, t + 1)
            for p in range(PAIRS):
                m = pe.matmul(b2[:, 2 * p:2 * p + 2], sq2[:, TILE * p:TILE * (p + 1)], cmean, start=True, stop=True)
            m.then_inc(var2_mm, 1)

        def pe_rstd2(pe, t):
            wait(pe, rrep_done, t + 1)
            for p in range(PAIRS):
                m = pe.transpose(b2[:, TILE * p:TILE * (p + 1)],
                                 rrep[:, 2 * p:2 * p + 2, :].rearrange("p a b -> p (a b)"), ident)
            m.then_inc(rstd2_mm, 1)

        rrep = sb("rrep", [P, B, C])
        rrep_done = sem("rrep_done")

        def pe_a(pe, t, e):
            if e == 0:
                wait(pe, tn2_done, t + 1)
            wait(pe, gelu_out, 2 * t + e + 1)
            half = slice(C * e, C * e + C)
            pe.matmul((b4, b6)[e][:, :], top["w1T"][half, :], tn2[half, :], start=True, stop=True).then_inc(a_mm, 1)

        def rows(ap, r):
            return ap.rearrange("p (q r w) -> p r q w", q=PAIRS, r=2)[:, r]

        def pe_cow(pe, t, e):
            half = slice(C * e, C * e + C)
            for r in range(2):
                dst = slice(C * (1 - r), C * (1 - r) + C)
                pe.matmul((b5, b7)[e][dst, 0:PAIRS * HW], top["cowT"][half, :], rows(z1[half, :], r),
                          start=True, stop=False)

        def pe_out(pe, t, e):
            wait(pe, gated_done, 2 * t + e + 1)
            for r in range(2):
                dst = slice(C * (1 - r), C * (1 - r) + C)
                m = pe.matmul((b5, b7)[e][dst, 0:PAIRS * HW], top["w3T"][:, :], rows(gated[e][:, :], r),
                              start=False, stop=True)
            m.then_inc(out_mm, 1)

        def act_raw(act, t, k, g):
            wait(act, qkv_mm, 4 * t + g + 1)
            if g == 0:
                wait(act, z1_mm, t - 1)
                wait(act, qkv_done, B * (t - 1))
            act.activation(traw[k][:, 2 * g:2 * g + 2, :], q_ps[g % 2][:, :, 0:C], ACT.Identity)
            act.activation(raw[k][:, 2 * g:2 * g + 2, C:4 * C], q_ps[g % 2][:, :, C:4 * C], ACT.Identity)\
                .then_inc(raw_out, 1)

        def act_scores_t(act, t):
            wait(act, scoresT_mm, t + 1)
            wait(act, scores_mm, t)
            act.activation(scoresT[:, :, :].rearrange("p a b -> p (a b)"), b2[:, :], ACT.Identity).then_inc(scoresT_out, 1)

        def act_z(act, t):
            wait(act, av_mm, t + 1)
            wait(act, z1_mm, t)
            act.activation(z[:, :], b4[:, :], ACT.Identity).then_inc(z_out, 1)

        def act_z1(act, t):
            wait(act, z1_mm, t + 1)
            act.activation(z1[:, :], b5[:, :], ACT.Identity, bias=cols[:, 1:2]).then_inc(z1_out, 1)

        def act_center(act, t):
            wait(act, cen2_mm, t + 1)
            wait(act, var2_mm, t)
            wait(act, tn2_done, t)
            act.activation(sq2[:, :], b4[:, :], ACT.Square).then_inc(sq2_out, 1)
            act.activation(cen2[:, :], b4[:, :], ACT.Identity).then_inc(cen2_out, 1)

        def act_exp(act, t):
            wait(act, shift_done, t + 1)
            wait(act, attn_done, t)
            wait(act, den_done, t)
            act.activation(exps[:, :], shifted[:, :], ACT.Exp, scale=float(HD) ** -0.5).then_inc(exp_out, 1)

        def act_gelu(act, t, e):
            wait(act, g_mm, 2 * t + e + 1)
            wait(act, gated_done, 2 * t + e - 1)
            act.activation(gel[e][:, :], (b6, b7)[e][:, :], ACT.Gelu, bias=cols[:, 3:4]).then_inc(gelu_out, 1)

        def dve_softmax_max(dve, t):
            wait(dve, scores_mm, t + 1)
            wait(dve, shift_done, t)
            view = b3[:, :].rearrange("p (i j h) -> p i h j", i=B, j=B)
            dve.tensor_reduce(smax[:, :].rearrange("p (i h) -> p i h", i=B), view, AX.X, ALU.max).then_inc(smax_done, 1)
            wait(dve, smax_done, t + 1)
            wait(dve, exp_out, t)
            top_of = smax[:, :].rearrange("p (i h) -> p i h", i=B).unsqueeze(2).broadcast_to([P, B, B, HEADS])
            dve.tensor_tensor(shifted[:, :].rearrange("p (i j h) -> p i j h", i=B, j=B),
                              b3[:, :].rearrange("p (i j h) -> p i j h", i=B, j=B), top_of, ALU.subtract)\
                .then_inc(shift_done, 1)

        def dve_softmax_sum(dve, t):
            wait(dve, exp_out, t + 1)
            wait(dve, rden_done, t)
            dve.tensor_reduce(den[:, :].rearrange("p (i h) -> p i h", i=B),
                              exps[:, :].rearrange("p (i j h) -> p i h j", i=B, j=B), AX.X, ALU.add).then_inc(den_done, 1)
            wait(dve, den_done, t + 1)
            wait(dve, attn_done, t)
            dve.reciprocal(rden[:, :], den[:, :]).then_inc(rden_done, 1)

        def dve_stats(dve, t, k, g):
            wait(dve, raw_out, 4 * t + g + 1)
            if g == 0:
                wait(dve, tiny_done, 5 * t)
            for i in (2 * g, 2 * g + 1):
                dve.bn_stats(st1[:, i, :], traw[k][:, i, :]).then_inc(stats_done, 1)

        def dve_var1(dve, t):
            wait(dve, stats_done, B * (t + 1))
            wait(dve, rstd1_done, t)
            dve.tensor_tensor(tiny[:, 0, :], st1[:, :, 1], st1[:, :, 4], ALU.subtract).then_inc(tiny_done, 1)
            dve.tensor_tensor(tiny[:, 1, :], st1[:, :, 2], st1[:, :, 5], ALU.add).then_inc(tiny_done, 1)
            wait(dve, tiny_done, 5 * t + 2)
            dve.scalar_tensor_tensor(tiny[:, 2, :], tiny[:, 0, :], C / 4.0, tiny[:, 0, :], ALU.mult, ALU.mult)\
                .then_inc(tiny_done, 1)
            wait(dve, tiny_done, 5 * t + 3)
            dve.tensor_tensor(tiny[:, 2, :], tiny[:, 2, :], tiny[:, 1, :], ALU.add).then_inc(tiny_done, 1)
            wait(dve, tiny_done, 5 * t + 4)
            dve.tensor_scalar(tiny[:, 3, :], tiny[:, 2, :], 1.0 / C, 1e-5, ALU.mult, ALU.add).then_inc(tiny_done, 1)

        def dve_qkv(dve, t, k):
            wait(dve, rstd1_done, t + 1)
            wait(dve, p2_pool, NP * (t - 1))
            wait(dve, p2_dve, ND * (t - 1))
            for i in range(B):
                dve.scalar_tensor_tensor(qkv[k][:, i, :], raw[k][:, i, C:4 * C], rstd1[:, i:i + 1], top["brep"][:, :],
                                         ALU.mult, ALU.add).then_inc(qkv_done, 1)

        def dve_p1(dve, t, k):
            wait(dve, qkv_done, B * (t + 1))
            wait(dve, scoresT_mm, t)
            for i in range(ND):
                p1_product(dve, k, i).then_inc(p1_dve, 1)

        def dve_rrep(dve, t):
            wait(dve, rstd2_done, t + 1)
            wait(dve, rstd2_mm, t)
            dve.tensor_scalar(rrep[:, :, :], rstd2[:, :].unsqueeze(2).broadcast_to([P, B, C]), 1.0, None, ALU.mult)\
                .then_inc(rrep_done, 1)

        def dve_p2(dve, t, k, js):
            wait(dve, attn_done, t + 1)
            wait(dve, av_mm, t)
            for j in js:
                p2_product(dve, k, j).then_inc(p2_dve, 1)

        def dve_var2(dve, t):
            wait(dve, var2_mm, t + 1)
            wait(dve, rstd2_done, t)
            dve.tensor_scalar(var2[:, :], b2[:, 0:B], 1e-5, None, ALU.add).then_inc(var2_done, 1)

        def dve_tn2(dve, t):
            wait(dve, rstd2_mm, t + 1)
            wait(dve, cen2_out, t + 1)
            wait(dve, a_mm, 2 * t)
            dve.tensor_tensor(tn2[:, :], b2[:, :], cen2[:, :], ALU.mult).then_inc(tn2_done, 1)

        def dve_gated(dve, t, e):
            wait(dve, a_mm, 2 * t + e + 1)
            wait(dve, gelu_out, 2 * t + e + 1)
            wait(dve, out_mm, 2 * t + e - 1)
            dve.scalar_tensor_tensor(gated[e][:, :], (b4, b6)[e][:, :], cols[:, 2:3], gel[e][:, :], ALU.add, ALU.mult)\
                .then_inc(gated_done, 1)

        def dve_x(dve, t, k):
            if isinstance(t, int):
                dve.wait_ge(xr_in[k], 32 * ((t - k) // 2 + 1))
            else:
                dve.wait_ge(xr_in[k], (t - k) * 16 + 32)
            for e in range(2):
                wait(dve, out_mm, 2 * t + e + 1)
                for r in range(2):
                    half = slice(C * (1 - r), C * (1 - r) + C)
                    dve.scalar_tensor_tensor(
                        xs[half, e::2, bass.ds(t + r, 1), :].rearrange("p q s w -> p q (s w)"),
                        (b5, b7)[e][half, 0:PAIRS * HW].rearrange("p (q w) -> p q w", q=PAIRS),
                        cols[half, 4:5], xr[k][half, e::2, :], ALU.add, ALU.add).then_inc(x_done, 1)

        def pool_rstd1(pool, t):
            wait(pool, tiny_done, 5 * t + 5)
            wait(pool, qkv_done, B * t)
            pool.tensor_tensor(rstd1[:, :], tiny[:, 3, :], top["half"][:, :], ALU.pow).then_inc(rstd1_done, 1)

        def pool_attn(pool, t):
            wait(pool, rden_done, t + 1)
            wait(pool, p2_dve, ND * t)
            wait(pool, p2_pool, NP * t)
            r = rden[:, :].rearrange("p (i h) -> p i h", i=B).unsqueeze(2).broadcast_to([P, B, B, HEADS])
            pool.tensor_tensor(attn[:, :].rearrange("p (i j h) -> p i j h", i=B, j=B),
                               exps[:, :].rearrange("p (i j h) -> p i j h", i=B, j=B), r, ALU.mult).then_inc(attn_done, 1)

        def pool_p2(pool, t, k, js):
            wait(pool, attn_done, t + 1)
            wait(pool, av_mm, t)
            for j in js:
                p2_product(pool, k, j).then_inc(p2_pool, 1)

        def pool_rstd2(pool, t):
            wait(pool, var2_done, t + 1)
            wait(pool, rrep_done, t)
            pool.tensor_tensor(rstd2[:, :], var2[:, :], top["half"][:, :], ALU.pow).then_inc(rstd2_done, 1)

        def pool_p1(pool, t, k):
            wait(pool, qkv_done, B * (t + 1))
            wait(pool, scoresT_mm, t)
            for i in range(ND, B):
                p1_product(pool, k, i).then_inc(p1_pool, 1)

        def sp_xt(sp, t, k):
            wait(sp, qkv_mm, 4 * (t - 1))
            src = x_flat[:, :, bass.ds(t * TILE, TILE)]
            sp.dma_start(top["xt"][k][0:C, :, :], src).then_inc(xt_in[k], 16)

        def sp_xr(sp, t, k):
            wait(sp, x_done, 4 * (t - 1))
            for r in range(2):
                half = slice(C * (1 - r), C * (1 - r) + C)
                sp.dma_start(xr[k][half, :, :],
                             x_rows[:, :, bass.ds(2 * t + r, 1), :].rearrange("c b r w -> c b (r w)")).then_inc(xr_in[k], 16)

        def pe_iteration(pe, t, k, fin, mid, new):
            if fin:
                pe_av(pe, t)
            if mid:
                pe_scores_t(pe, t + 1)
            if fin:
                pe_z1(pe, t, k)
            if mid:
                pe_scores(pe, t + 1)
            if new:
                for g in range(3):
                    pe_qkv(pe, t + 2, k, g)
            if fin:
                pe_center(pe, t)
            if new:
                pe_qkv(pe, t + 2, k, 3)
            if fin:
                pe_g(pe, t, 0)
                pe_var2(pe, t)
                pe_g(pe, t, 1)
                pe_cow(pe, t, 0)
                pe_rstd2(pe, t)
                pe_a(pe, t, 0)
                pe_a(pe, t, 1)
                pe_cow(pe, t, 1)
                pe_out(pe, t, 0)
                pe_out(pe, t, 1)

        def act_iteration(act, t, k, fin, mid, new):
            if fin:
                act_z(act, t)
            if mid:
                act_scores_t(act, t + 1)
            if fin:
                act_z1(act, t)
            if new:
                act_raw(act, t + 2, k, 0)
                act_raw(act, t + 2, k, 1)
            if mid:
                act_exp(act, t + 1)
            if fin:
                act_center(act, t)
            if new:
                act_raw(act, t + 2, k, 2)
                act_raw(act, t + 2, k, 3)
            if fin:
                act_gelu(act, t, 0)
                act_gelu(act, t, 1)

        def dve_iteration(dve, t, k, fin, mid, new):
            if mid:
                dve_softmax_max(dve, t + 1)
            if new:
                dve_stats(dve, t + 2, k, 0)
                dve_stats(dve, t + 2, k, 1)
            if mid:
                dve_softmax_sum(dve, t + 1)
            if new:
                dve_stats(dve, t + 2, k, 2)
                dve_stats(dve, t + 2, k, 3)
                dve_var1(dve, t + 2)
            if fin:
                dve_var2(dve, t)
            if mid:
                dve_p2(dve, t + 1, 1 - k, range(0, 2))
            if fin:
                dve_rrep(dve, t)
            if mid:
                dve_p2(dve, t + 1, 1 - k, range(2, ND))
            if fin:
                dve_tn2(dve, t)
            if new:
                dve_qkv(dve, t + 2, k)
            if fin:
                dve_gated(dve, t, 0)
                dve_gated(dve, t, 1)
            if new:
                dve_p1(dve, t + 2, k)
            if fin:
                dve_x(dve, t, k)

        def pool_iteration(pool, t, k, fin, mid, new):
            if mid:
                pool_attn(pool, t + 1)
            if new:
                pool_rstd1(pool, t + 2)
            if fin:
                pool_rstd2(pool, t)
            if mid:
                pool_p2(pool, t + 1, 1 - k, range(ND, B))
            if new:
                pool_p1(pool, t + 2, k)

        def sp_iteration(sp, t, k, fin, mid, new):
            if new:
                if not isinstance(t, int) or t + 4 < TILES:
                    sp_xt(sp, t + 4, k)
                sp_xr(sp, t + 2, k)

        def run(eng, iteration):
            for t in range(-2, 2):
                iteration(eng, t, t % 2, t >= 0, t >= -1, True)
            with eng.Fori(1, TILES // 2 - 2) as pair:
                for k in range(2):
                    iteration(eng, pair * 2 + k, k, True, True, True)
            for t in range(TILES - 4, TILES):
                iteration(eng, t, t % 2, True, t + 1 < TILES, t + 2 < TILES)

        block = ctx.enter_context(nc.Block())

        @block.tensor
        def _(pe):
            run(pe, pe_iteration)

        @block.scalar
        def _(act):
            run(act, act_iteration)

        @block.vector
        def _(dve):
            run(dve, dve_iteration)

        @block.gpsimd
        def _(pool):
            run(pool, pool_iteration)

        @block.sync
        def _(sp):
            sp_xt(sp, 0, 0)
            sp_xt(sp, 1, 1)
            run(sp, sp_iteration)


def conv_steps(nc, d, top):
    with ExitStack() as ctx:
        def sb(name, shape, dt=F32):
            return ctx.enter_context(nc.sbuf_tensor(name, shape, dt))

        def sem(name):
            return ctx.enter_context(nc.semaphore(name))

        xs, cols = top["xs"], top["cols"]
        a_hi, a_lo = (sb(n, [P, SLOTS, PADW], F32R) for n in ("a_hi", "a_lo"))
        m_hi, m_lo = (sb(n, [P, SLOTS + 1, PADW], F32R) for n in ("m_hi", "m_lo"))
        RING = 3
        evac = [sb(f"evac{k}", [P, 8, HW]) for k in range(RING)]
        result = sb("result", [P, SLOTS, HW])
        banks = [ctx.enter_context(nc.psum_tensor(f"conv{k}", [P, 8, HW], F32)) for k in range(8)]
        zeroed, conv_mm, evac_out, split_x, split_m = sem("zeroed"), sem("conv_mm"), sem("evac_out"), sem("split_x"), sem("split_m")
        x_added, hi_done, result_done, stored = sem("x_added"), sem("hi_done"), sem("result_done"), sem("stored")

        QA = [(8 * q, 8) for q in range(4)] + [(SLOTS - 1, 1)]
        QM = [(8 * q, 8) for q in range(4)]
        PER_STEP = len(QA) + len(QM)
        PER_IMAGE = STEPS * PER_STEP
        tiles = [(s, c, q) for s in range(STEPS) for c in range(2) for q in range(len((QM, QA)[c]))]
        NA, NM = len(QA), len(QM)

        def bank_free(n):
            before = [k for k in range(n) if k % 8 == n % 8]
            return before[-1] + 1 if before else [k for k in range(PER_IMAGE) if k % 8 == n % 8][-1] + 1 - PER_IMAGE

        def pe_image(pe, img, first):
            for n, (s, c, q) in enumerate(tiles):
                base = img * PER_IMAGE
                need = bank_free(n)
                if not (first and need <= 0):
                    pe.wait_ge(evac_out, base + need)
                if c == 0:
                    pe.wait_ge(split_x, img * (NA * STEPS) + (NA * s + q + 2))
                else:
                    pe.wait_ge(split_m, img * (NM * STEPS) + (NM * s + min(q + 1, NM)))
                s0, cnt = (QM, QA)[c][q]
                hi, lo = ((a_hi, a_lo), (m_hi, m_lo))[c]
                wh, wl = top["cwh"][c], top["cwl"][c]
                k = 0
                for slot in range(2):
                    for kx in range(TAPS):
                        for w, v in ((wh, hi), (wh, lo), (wl, hi)):
                            m = pe.matmul(banks[n % 8][:, 0:cnt, :], w[:, slot, kx, :],
                                          v[:, s0 + slot:s0 + slot + cnt, kx:kx + HW],
                                          start=(k == 0), stop=(k == 6 * TAPS - 1))
                            k += 1
                m.then_inc(conv_mm, 1)

        def act_image(act, img, first):
            for n, (s, c, q) in enumerate(tiles):
                act.wait_ge(conv_mm, img * PER_IMAGE + n + 1)
                s0, cnt = (QM, QA)[c][q]
                if not (first and n < RING):
                    act.wait_ge(*freed(img, n))
                if c == 0:
                    act.activation(evac[n % RING][:, 0:cnt, :], banks[n % 8][:, 0:cnt, :], ACT.Relu,
                                   bias=cols[:, 6:7]).then_inc(evac_out, 1)
                else:
                    act.activation(evac[n % RING][:, 0:cnt, :], banks[n % 8][:, 0:cnt, :], ACT.Identity,
                                   bias=cols[:, 8:9], scale=H_STEP).then_inc(evac_out, 1)

        def freed(img, n):
            k = n - RING
            back = 0 if k >= 0 else 1
            s, c, q = tiles[k % PER_IMAGE]
            if c == 0:
                return split_m, (img * (NM * STEPS)) + (NM * s + q + 1 - back * NM * STEPS)
            return x_added, (img * (XA * STEPS)) + (XA * s + adds(q + 1) - back * XA * STEPS)

        XA = NA + 1

        def adds(q):
            return q + 1 if q else 0

        def split(dve, src, hi, lo, img, count, what):
            dve.tensor_scalar(hi, src, 1.0, None, ALU.mult).then_inc(hi_done, 1)
            dve.wait_ge(hi_done, count)
            dve.tensor_tensor(lo, src, hi.bitcast(F32), ALU.subtract).then_inc(what, 1)

        HI = (NA + NM) * STEPS

        def x_of(img, s0, cnt):
            return xs[:, bass.ds(img, 1), s0:s0 + cnt, :].rearrange("p b s w -> p (b s) w")

        def first_split(dve, img, n0):
            for q, (s0, cnt) in enumerate(QA):
                split(dve, x_of(img, s0, cnt), a_hi[:, s0:s0 + cnt, 1:1 + HW], a_lo[:, s0:s0 + cnt, 1:1 + HW],
                      img, img * HI + (n0 + q + 1), split_x)

        def dve_image(dve, img, last):
            h = NA
            x_adds = 0
            for n, (s, c, q) in enumerate(tiles):
                s0, cnt = (QM, QA)[c][q]
                dve.wait_ge(evac_out, img * PER_IMAGE + n + 1)
                src = evac[n % RING][:, 0:cnt, :]
                if c == 0:
                    h += 1
                    split(dve, src, m_hi[:, s0 + 1:s0 + 1 + cnt, 1:1 + HW], m_lo[:, s0 + 1:s0 + 1 + cnt, 1:1 + HW],
                          img, img * HI + h, split_m)
                    if s == STEPS - 1 and q == NM - 1 and not last:
                        first_split(dve, img + 1, 0)
                    continue
                parts = [(slice(0, P), s0, cnt)]
                if q == 0:
                    parts = [(slice(C, P), 0, 1), (slice(0, P), 1, cnt - 1)]
                if q == NA - 1:
                    parts = [(slice(0, C), s0, 1)]
                for part, p0, pc in parts:
                    x_adds += 1
                    xv = xs[part, bass.ds(img, 1), p0:p0 + pc, :].rearrange("p b s w -> p (b s) w")
                    dve.tensor_tensor(xv, xv, evac[n % RING][part, p0 - s0:p0 - s0 + pc, :], ALU.add).then_inc(x_added, 1)
                dve.wait_ge(x_added, img * (XA * STEPS) + x_adds)
                if s < STEPS - 1:
                    h += 1
                    split(dve, x_of(img, s0, cnt), a_hi[:, s0:s0 + cnt, 1:1 + HW], a_lo[:, s0:s0 + cnt, 1:1 + HW],
                          img, img * HI + h, split_x)
                else:
                    if q == 0 and not (isinstance(img, int) and img == 0):
                        dve.wait_ge(stored, img * STORED)
                    dve.tensor_scalar(result[:, s0:s0 + cnt, :], x_of(img, s0, cnt), 0.0, None, ALU.max)\
                        .then_inc(result_done, 1)

        out = d["out"].rearrange("b c (p r) w -> b r c p w", r=2)
        STORED = 16 * 2 * NM

        def sp_image(sp, img):
            for q in range(NM):
                sp.wait_ge(result_done, img * NA + q + 2)
                s0 = 8 * q
                sp.dma_start(out[bass.ds(img, 1), 0, :, s0:s0 + 8, :].rearrange("b c p w -> (b c) p w"),
                             result[C:P, s0:s0 + 8, :]).then_inc(stored, 16)
                sp.dma_start(out[bass.ds(img, 1), 1, :, s0:s0 + 8, :].rearrange("b c p w -> (b c) p w"),
                             result[0:C, s0 + 1:s0 + 9, :]).then_inc(stored, 16)

        block = ctx.enter_context(nc.Block())

        @block.tensor
        def _(pe):
            pe.wait_ge(zeroed, 6)
            pe_image(pe, 0, True)
            with pe.Fori(1, B) as img:
                pe_image(pe, img, False)

        @block.scalar
        def _(act):
            act_image(act, 0, True)
            with act.Fori(1, B) as img:
                act_image(act, img, False)

        @block.vector
        def _(dve):
            for t in (a_hi, a_lo, m_hi, m_lo):
                dve.memset(t[:, :, :].bitcast(F32), 0.0).then_inc(zeroed, 1)
            dve.memset(xs[0:C, :, 0, :], 0.0).then_inc(zeroed, 1)
            dve.memset(xs[C:P, :, SLOTS - 1, :], 0.0).then_inc(zeroed, 1)
            dve.wait_ge(zeroed, 6)
            first_split(dve, 0, 0)
            dve_image(dve, 0, False)
            with dve.Fori(1, B - 1) as img:
                dve_image(dve, img, False)
            dve_image(dve, B - 1, True)

        @block.sync
        def _(sp):
            with sp.Fori(0, B) as img:
                sp_image(sp, img)
            sp.wait_ge(stored, STORED * B)


def program(nc, d):
    with ExitStack() as ctx:
        def sb(name, shape, dt=F32):
            return ctx.enter_context(nc.sbuf_tensor(name, shape, dt))

        top = {
            "consts": sb("consts", [P, K_END]),
            "cols": sb("cols", [P, 9]),
            "half": sb("half", [P, B]),
            "xt": [sb(f"xt{k}", [C + 1, B, TILE]) for k in range(2)],
            "wcat": sb("wcat", [C + 1, B, 4 * C]),
            "woutT": sb("woutT", [P, P]), "cowT": sb("cowT", [P, C]),
            "w1T": sb("w1T", [P, HID]), "w2T": sb("w2T", [P, HID]), "w3T": sb("w3T", [HID, C]),
            "brep": sb("brep", [P, 3 * C]),
            "cwh": [sb(f"cwh{k}", [P, 2, TAPS, P], F32R) for k in range(2)],
            "cwl": [sb(f"cwl{k}", [P, 2, TAPS, P], F32R) for k in range(2)],
            "xs": sb("xs", [P, B, SLOTS, HW]),
        }
        setup_weights(nc, d, None, top)
        attention_block(nc, d, top)
        conv_steps(nc, d, top)


_INS = ["x"] + ["L0_conv_" + n for n in (
    "gn_g gn_b ciw cib pe ln1g ln1b wq bq wk bk wv bv win bin_ wout bout ln2g ln2b w1 b1 w2 b2 w3 b3 cow cob").split()] \
    + ["L1_conv_" + n for n in "w1 b1 w2 b2".split()]


def kernel(**inputs):
    import numpy as np
    import concourse.bacc as bacc
    from concourse import mybir as mb
    from concourse.bass_utils import run_bass_kernel_spmd

    consts = np.zeros((P, K_END), np.float32)
    consts[:, K_ID:K_ID + P] = np.eye(P)
    for k in range(2):
        half = slice(C * k, C * k + C)
        consts[half, K_CEN + C * k:K_CEN + C * k + C] = np.eye(C) - 1.0 / C
        consts[half, K_MEAN + k] = 1.0 / C
    for g in range(P // 8):
        consts[8 * g:8 * g + 8, K_GRP + 8 * g:K_GRP + 8 * g + 8] = 1.0 / 8

    nc = bacc.Bacc("TRN2", target_bir_lowering=False, num_devices=1)
    arrays, d = {}, {}
    for name in _INS:
        a = np.ascontiguousarray(inputs[name])
        arrays[f"in_{name}"] = a
        d[name] = nc.dram_tensor(f"in_{name}", a.shape, mb.dt.from_np(a.dtype), kind="ExternalInput").ap()
    arrays["in_consts"] = consts
    d["consts"] = nc.dram_tensor("in_consts", consts.shape, mb.dt.float32, kind="ExternalInput").ap()
    d["out"] = nc.dram_tensor("out_y", (B, C, HW, HW), mb.dt.float32, kind="ExternalOutput").ap()
    program(nc, d)
    r = run_bass_kernel_spmd(nc, [arrays], core_ids=[0])
    return r.results[0]["out_y"]
```

```python
import concourse.bass as bass
from concourse import mybir
from contextlib import ExitStack

B, C, HW = 8, 64, 64
HEADS = 8
HD = C // HEADS
HID = 2 * C
PIX = HW * HW
TILE = 2 * HW
TILES = PIX // TILE
PAIRS = B // 2
P = 2 * C
SLOTS = HW // 2 + 1
PADW = HW + 2
STEPS = 3
H_STEP = 1.0 / 3.0
TAPS = 3
POOL_I = 3
F32, F32R = mybir.dt.float32, mybir.dt.float32r
ALU, ACT, AX = mybir.AluOpType, mybir.ActivationFunctionType, mybir.AxisListType
K_ID, K_CEN, K_GRP, K_MEAN, K_END = 0, P, 2 * P, 3 * P, 4 * P


def wait(eng, sem, n):
    if isinstance(n, int) and n <= 0:
        return
    eng.wait_ge(sem, n)


def setup_weights(nc, d, s, top):
    with ExitStack() as ctx:
        def sb(name, shape, dt=F32):
            return ctx.enter_context(nc.sbuf_tensor(name, shape, dt))

        def ps(name, shape):
            return ctx.enter_context(nc.psum_tensor(name, shape, F32))

        def sem(name):
            return ctx.enter_context(nc.semaphore(name))

        win = sb("win", [C, 3, C])
        wqkv = sb("wqkv", [C, 3, C])
        ciw = sb("ciw", [C, C])
        wout2 = sb("wout2", [C, 2, C])
        cow2 = sb("cow2", [C, 2, C])
        w1n = sb("w1n", [HID, 2, C])
        w2n = sb("w2n", [HID, 2, C])
        w3n = sb("w3n", [C, HID])
        binr = sb("binr", [1, 3 * C])
        ones1 = sb("ones1", [1, P])
        vec = sb("vec", [C, 12])
        pen = sb("pen", [B, C])
        pet = sb("pet", [C, B])
        cw = [sb(f"cw{k}", [C, C, TAPS * TAPS]) for k in range(2)]
        cw2 = sb("cw2", [C, TAPS * TAPS, 2, C])
        wiT = sb("wiT", [C, 3, C])
        rq = sb("rq", [C, 3 * C])
        rqg = sb("rqg", [C, 3 * C])
        basis = sb("basis", [C, 4 * C])
        reps = sb("reps", [C, 4, P])
        w1raw = sb("w1raw", [P, HID])
        wall = sb("wall", [C, 4 * C])
        cowrep = sb("cowrep", [C, 2, C])
        convf = sb("convf", [P, 2, TAPS, P])
        xst = [sb(f"xst{k}", [P, PIX]) for k in range(2)]
        st = sb("st", [P, 8, 6])
        mv = sb("mv", [P, PAIRS, 2])
        means = sb("means", [P, PAIRS])
        dev = sb("dev", [P, PAIRS])
        wvar = sb("wvar", [P, PAIRS])
        mu = sb("mu", [C, B])
        gvar = sb("gvar", [C, B])
        gexp = sb("gexp", [C, B])
        ga = sb("ga", [C, B])
        gb = sb("gb", [C, B])
        cvec = sb("cvec", [C, B])
        beta = sb("beta", [B, 4 * C])
        pt = [ps(f"pset{k}", [P, 512]) for k in range(8)]

        loaded, xin, pe_done, dve_done = sem("loaded"), [sem("xin0"), sem("xin1")], sem("pe_done"), sem("dve_done")
        rs_ready, beta_moved = sem("rs_ready"), sem("beta_moved")
        GN_G, GN_B, LN1G, LN1B, BQ, BK, BV, CIB, B3, LN2B = range(10)
        ident, center = top["consts"][:, K_ID:K_ID + P], top["consts"][:, K_CEN:K_CEN + P]
        group = top["consts"][:, K_GRP:K_GRP + P]

        loads = [
            (top["consts"][:, :], d["consts"]),
            (win[:, :, :], d["L0_conv_win"].rearrange("(t o) i -> o t i", t=3)),
            (wqkv[:, 0, :], d["L0_conv_wq"]), (wqkv[:, 1, :], d["L0_conv_wk"]), (wqkv[:, 2, :], d["L0_conv_wv"]),
            (ciw[:, :], d["L0_conv_ciw"]), (w3n[:, :], d["L0_conv_w3"]),
            (binr[:, :], d["L0_conv_bin_"].rearrange("(a n) -> a n", a=1)),
            (pen[:, :], d["L0_conv_pe"][0:B, :]),
        ]
        for k in range(2):
            loads += [(wout2[:, k, :], d["L0_conv_wout"]), (cow2[:, k, :], d["L0_conv_cow"]),
                      (w1n[:, k, :], d["L0_conv_w1"]), (w2n[:, k, :], d["L0_conv_w2"]),
                      (cw[k][:, :, :], d[f"L1_conv_w{k + 1}"].rearrange("o i a b -> o i (a b)"))]
            half = slice(C * k, C * k + C)
            for col, name in ((0, "L0_conv_ln2g"), (1, "L0_conv_bout"), (4, "L0_conv_cob"),
                              (6, "L1_conv_b1"), (7, "L1_conv_b2")):
                loads.append((top["cols"][half, col:col + 1], d[name].rearrange("(n a) -> n a", a=1)))
        for col, name in ((2, "L0_conv_b1"), (3, "L0_conv_b2")):
            loads.append((top["cols"][:, col:col + 1], d[name].rearrange("(n a) -> n a", a=1)))
        for col, name in ((GN_G, "L0_conv_gn_g"), (GN_B, "L0_conv_gn_b"), (LN1G, "L0_conv_ln1g"),
                          (LN1B, "L0_conv_ln1b"), (BQ, "L0_conv_bq"), (BK, "L0_conv_bk"), (BV, "L0_conv_bv"),
                          (CIB, "L0_conv_cib"), (B3, "L0_conv_b3"), (LN2B, "L0_conv_ln2b")):
            loads.append((vec[:, col:col + 1], d[name].rearrange("(n a) -> n a", a=1)))
        all_loaded = 16 * len(loads)
        at = {}

        block = ctx.enter_context(nc.Block())

        def x_pair(p):
            return d["x"][2 * p:2 * p + 2].rearrange("b c h w -> (b c) (h w)")

        @block.vector
        def _(dve):
            n = [0]

            def link(ins, name=None):
                n[0] += 1
                ins.then_inc(dve_done, 1)
                dve.wait_ge(dve_done, n[0])
                if name:
                    at[name] = n[0]

            link(dve.memset(ones1[:, :], 1.0))
            link(dve.memset(gexp[:, :], -0.5))
            link(dve.memset(top["half"][:, :], -0.5))
            for k in range(2):
                link(dve.memset(top["xt"][k][C:C + 1, :, :], 1.0))
            link(dve.memset(top["woutT"][:, :], 0.0), "zeros")
            dve.wait_ge(loaded, all_loaded)
            for k, col in enumerate((LN1B, BQ, BK, BV)):
                link(dve.tensor_copy(reps[:, k, :], vec[:, col:col + 1].broadcast_to([C, P])))
            dve.wait_ge(pe_done, 1)
            link(dve.tensor_copy(wiT[:, :, :], pt[0][0:C, 0:3 * C].rearrange("p (t o) -> p t o", t=3)), "wiT")
            dve.wait_ge(pe_done, 2)
            for k in range(2):
                half = slice(C * k, C * k + C)
                link(dve.tensor_copy(top["woutT"][half, half], pt[1][half, 0:C]))
            link(dve.tensor_copy(pet[:, :], pt[1][0:C, 2 * C:2 * C + B]))
            link(dve.tensor_copy(top["cowT"][:, :], pt[1][:, C:2 * C]))
            for k in range(2):
                link(dve.tensor_copy(cowrep[:, k, :], pt[1][0:C, C:2 * C]), "cowT")
            dve.wait_ge(pe_done, 3)
            link(dve.tensor_copy(w1raw[:, :], pt[2][:, 0:HID]))
            link(dve.tensor_scalar(top["w1T"][:, :], pt[2][:, 0:HID], top["cols"][:, 0:1], None, ALU.mult))
            link(dve.tensor_copy(top["w2T"][:, :], pt[2][:, HID:2 * HID]), "w1raw")
            dve.wait_ge(pe_done, 4)
            link(dve.tensor_copy(rq[:, :], pt[3][0:C, 0:3 * C]))
            link(dve.tensor_scalar(rqg[:, :], pt[3][0:C, 0:3 * C], vec[:, LN1G:LN1G + 1], None, ALU.mult), "rq")
            dve.wait_ge(pe_done, 6)
            link(dve.tensor_copy(basis[:, 0:C], ident[0:C, 0:C]))
            for k in range(2):
                cols = slice(C * (k + 1), C * (k + 2))
                link(dve.tensor_copy(basis[:, cols].rearrange("p (e h) -> p e h", h=HEADS),
                                     pt[4][0:C, C * k:C * (k + 1)].rearrange("p (h e) -> p e h", h=HEADS)))
                link(dve.tensor_copy(top["brep"][:, C * k:C * (k + 1)].rearrange("p (e h) -> p e h", h=HEADS),
                                     pt[5][:, C * k:C * (k + 1)].rearrange("p (h e) -> p e h", h=HEADS)))
            link(dve.tensor_copy(basis[:, 3 * C:4 * C], pt[4][0:C, 2 * C:3 * C]))
            link(dve.tensor_copy(top["brep"][:, 2 * C:3 * C], pt[5][:, 2 * C:3 * C]), "basis")
            dve.wait_ge(pe_done, 7)
            link(dve.tensor_copy(wall[:, :], pt[0][0:C, 0:4 * C]), "wall")
            dve.wait_ge(pe_done, 8)
            link(dve.tensor_copy(top["w3T"][:, :], pt[1][:, 0:C]))
            dve.wait_ge(pe_done, 9)
            link(dve.tensor_tensor(top["cols"][:, 4:5], pt[2][:, 0:1], top["cols"][:, 4:5], ALU.add))
            link(dve.tensor_tensor(top["cols"][:, 2:3], pt[2][:, 8:9], top["cols"][:, 2:3], ALU.add))
            link(dve.tensor_scalar(top["cols"][:, 8:9], top["cols"][:, 7:8], H_STEP, None, ALU.mult), "small")
            for k in range(2):
                link(dve.tensor_copy(cw2[:, :, 0, :], cw[k][:, :, :].rearrange("o i t -> o t i")))
                link(dve.tensor_copy(cw2[:, :, 1, :], cw[k][:, :, :].rearrange("o i t -> o t i")), f"cw{k}")
                link(dve.memset(convf[:, :, :, :], 0.0))
                dve.wait_ge(pe_done, 10 + k)
                for ky in range(TAPS):
                    for a in range(2):
                        for b in range(2):
                            for slot in range(2):
                                if 2 * slot + a - b == ky:
                                    ra, rb = slice(C * a, C * a + C), slice(C * b, C * b + C)
                                    link(dve.tensor_copy(
                                        convf[ra, slot, :, rb],
                                        pt[3 + ky][ra, 0:TAPS * C].rearrange("p (t o) -> p t o", t=TAPS)), f"cwout{k}")
                link(dve.tensor_copy(top["cwh"][k][:, :, :, :], convf[:, :, :, :]))
                link(dve.tensor_tensor(top["cwl"][k][:, :, :, :], convf[:, :, :, :],
                                       top["cwh"][k][:, :, :, :].bitcast(F32), ALU.subtract))
            for p in range(PAIRS):
                dve.wait_ge(xin[p % 2], 16 * (p // 2 + 1))
                for q in range(8):
                    link(dve.bn_stats(st[:, q, :], xst[p % 2][:, 512 * q:512 * (q + 1)]), f"x{p}")
                link(dve.bn_aggr(mv[:, p, :], st[:, :, :]))
            link(dve.tensor_copy(means[:, :], mv[:, :, 0]), "means")
            dve.wait_ge(pe_done, 12)
            link(dve.tensor_tensor(dev[:, :], means[:, :], pt[6][:, 0:PAIRS], ALU.subtract))
            link(dve.tensor_tensor(dev[:, :], dev[:, :], dev[:, :], ALU.mult))
            link(dve.tensor_tensor(wvar[:, :], mv[:, :, 1], dev[:, :], ALU.add), "wvar")
            dve.wait_ge(pe_done, 13)
            link(dve.tensor_copy(mu[:, :].rearrange("c (p e) -> c e p", e=2),
                                 pt[7][0:C, 0:B].rearrange("c (e p) -> c e p", e=2)))
            link(dve.tensor_scalar(gvar[:, :].rearrange("c (p e) -> c e p", e=2),
                                   pt[7][0:C, B:2 * B].rearrange("c (e p) -> c e p", e=2), 1e-6, None, ALU.add), "gvar")
            dve.wait_ge(rs_ready, 1)
            link(dve.tensor_scalar(ga[:, :], ga[:, :], vec[:, GN_G:GN_G + 1], None, ALU.mult))
            link(dve.tensor_tensor(mu[:, :], mu[:, :], ga[:, :], ALU.mult))
            link(dve.tensor_scalar(gb[:, :], mu[:, :], -1.0, vec[:, GN_B:GN_B + 1], ALU.mult, ALU.add), "gb")
            for i in range(B):
                link(dve.tensor_scalar(top["wcat"][0:C, i, :], wall[:, :], ga[:, i:i + 1], None, ALU.mult))
            dve.wait_ge(pe_done, 14)
            link(dve.scalar_tensor_tensor(cvec[:, :], pt[0][0:C, 0:B], vec[:, CIB:CIB + 1], pet[:, :],
                                          ALU.add, ALU.add), "cvec")
            dve.wait_ge(pe_done, 15)
            link(dve.tensor_copy(beta[:, :], pt[1][0:B, 0:4 * C]), "beta")

        @block.sync
        def _(sp):
            for k, (dst, src) in enumerate(loads):
                if k % 2 == 0:
                    sp.dma_start(dst, src).then_inc(loaded, 16)
            for p in range(PAIRS):
                if p >= 2:
                    sp.wait_ge(dve_done, at[f"x{p - 2}"])
                sp.dma_start(xst[p % 2][:, :], x_pair(p)).then_inc(xin[p % 2], 16)
            sp.wait_ge(dve_done, at["beta"])
            sp.dma_start(top["wcat"][C:C + 1, :, :], beta[:, :]).then_inc(beta_moved, 16)
            sp.wait_ge(beta_moved, 16)

        @block.scalar
        def _(act):
            for k, (dst, src) in enumerate(loads):
                if k % 2 == 1:
                    act.dma_start(dst, src).then_inc(loaded, 16)

        @block.gpsimd
        def _(pool):
            pool.wait_ge(dve_done, at["gvar"])
            pool.tensor_tensor(ga[:, :], gvar[:, :], gexp[:, :], ALU.pow).then_inc(rs_ready, 1)

        @block.tensor
        def _(pe):
            def need(name):
                pe.wait_ge(dve_done, at[name])

            pe.wait_ge(loaded, all_loaded)
            for t in range(3):
                m = pe.transpose(pt[0][0:C, C * t:C * (t + 1)], win[:, t, :], ident[0:C, 0:C])
            m.then_inc(pe_done, 1)
            pe.transpose(pt[1][:, 0:C], wout2[:, :, :].rearrange("p a b -> p (a b)"), ident[0:C, 0:C])
            pe.transpose(pt[1][0:C, 2 * C:2 * C + B], pen[:, :], ident[0:B, 0:B])
            pe.transpose(pt[1][:, C:2 * C], cow2[:, :, :].rearrange("p a b -> p (a b)"),
                         ident[0:C, 0:C]).then_inc(pe_done, 1)
            pe.transpose(pt[2][:, 0:HID], w1n[:, :, :].rearrange("p a b -> p (a b)"), ident)
            pe.transpose(pt[2][:, HID:2 * HID], w2n[:, :, :].rearrange("p a b -> p (a b)"),
                         ident).then_inc(pe_done, 1)
            need("wiT")
            for t in range(3):
                m = pe.matmul(pt[3][0:C, C * t:C * (t + 1)], wqkv[:, t, :], wiT[:, t, :], start=True, stop=True)
            m.then_inc(pe_done, 1)
            need("rq")
            pe.matmul(pt[4][0:C, 0:3 * C], center[0:C, 0:C], rqg[:, :], start=True, stop=True).then_inc(pe_done, 1)
            pe.matmul(pt[5][:, 0:3 * C], reps[:, 0, :], rq[:, :], start=True, stop=False)
            for t in range(3):
                pe.matmul(pt[5][:, C * t:C * (t + 1)], reps[:, 1 + t, :], wiT[:, t, :], start=False, stop=False)
            pe.matmul(pt[5][:, 0:3 * C], ones1[:, :], binr[:, :], start=False, stop=True).then_inc(pe_done, 1)
            need("basis")
            pe.matmul(pt[0][0:C, 0:4 * C], ciw[:, :], basis[:, :], start=True, stop=True).then_inc(pe_done, 1)
            need("cowT")
            pe.matmul(pt[1][:, 0:C], w3n[:, :], top["cowT"][0:C, :], start=True, stop=True).then_inc(pe_done, 1)
            need("w1raw")
            pe.matmul(pt[2][:, 0:1], cowrep[:, :, :].rearrange("p a b -> p (a b)"), vec[:, B3:B3 + 1],
                      start=True, stop=True)
            pe.matmul(pt[2][:, 8:9], w1raw[0:C, :], vec[:, LN2B:LN2B + 1], start=True, stop=True)\
                .then_inc(pe_done, 1)
            for k in range(2):
                need(f"cw{k}")
                if k:
                    need("cwout0")
                for ky in range(TAPS):
                    for kx in range(TAPS):
                        m = pe.transpose(pt[3 + ky][:, C * kx:C * (kx + 1)],
                                         cw2[:, TAPS * ky + kx, :, :].rearrange("p a b -> p (a b)"), ident[0:C, 0:C])
                m.then_inc(pe_done, 1)
            need("means")
            pe.matmul(pt[6][:, 0:PAIRS], group, means[:, :], start=True, stop=True).then_inc(pe_done, 1)
            need("wvar")
            for k, src in enumerate((means, wvar)):
                for e in range(2):
                    m = pe.matmul(pt[7][0:C, B * k + PAIRS * e:B * k + PAIRS * (e + 1)], group[:, C * e:C * (e + 1)],
                                  src[:, :], start=True, stop=True)
            m.then_inc(pe_done, 1)
            need("gb")
            pe.matmul(pt[0][0:C, 0:B], wall[:, 0:C], gb[:, :], start=True, stop=True).then_inc(pe_done, 1)
            need("cvec")
            pe.matmul(pt[1][0:B, 0:4 * C], cvec[:, :], basis[:, :], start=True, stop=True).then_inc(pe_done, 1)


def attention_block(nc, d, top):
    with ExitStack() as ctx:
        def sb(name, shape, dt=F32):
            return ctx.enter_context(nc.sbuf_tensor(name, shape, dt))

        def ps(name, shape):
            return ctx.enter_context(nc.psum_tensor(name, shape, F32))

        def sem(name):
            return ctx.enter_context(nc.semaphore(name))

        N = PAIRS * TILE
        S = B * B * HEADS
        raw = [sb(f"raw{k}", [P, B, 4 * C]) for k in range(2)]
        qkv = [sb(f"qkv{k}", [P, B, 3 * C]) for k in range(2)]
        xr = [sb(f"xr{k}", [P, B, HW]) for k in range(2)]
        prod1 = sb("prod1", [P, HD, S])
        prod2 = sb("prod2", [P, B, B * C])
        st1 = sb("st1", [P, B, 6])
        tiny = sb("tiny", [P, 4, B])
        rstd1 = sb("rstd1", [P, B])
        rstd2 = sb("rstd2", [P, B])
        var2 = sb("var2", [P, B])
        scoresT = sb("scoresT", [P, 4, P])
        smax = sb("smax", [P, C])
        shifted = sb("shifted", [P, S])
        exps = sb("exps", [P, S])
        den = sb("den", [P, C])
        rden = sb("rden", [P, C])
        attn = sb("attn", [P, S])
        z = sb("z", [P, N])
        z1 = [sb(f"z1_{k}", [P, N]) for k in range(2)]
        cen2 = sb("cen2", [P, N])
        sq2 = sb("sq2", [P, N])
        tn2 = sb("tn2", [P, N])
        gel = [sb(f"gel{e}", [P, N]) for e in range(2)]
        gated = [sb(f"gated{e}", [P, N]) for e in range(2)]

        q_ps = [ps(f"q_ps{k}", [P, 2, 4 * C]) for k in range(2)]
        b2 = ps("b2", [P, 512])
        b3 = ps("b3", [P, 512])
        b4 = ps("b4", [P, 512])
        b5 = ps("b5", [P, 512])
        b6 = ps("b6", [P, 512])
        b7 = ps("b7", [P, 512])

        xt_in = [sem("xt_in0"), sem("xt_in1")]
        xr_in = [sem("xr_in0"), sem("xr_in1")]
        qkv_mm, scoresT_mm, scores_mm, av_mm = sem("qkv_mm"), sem("scoresT_mm"), sem("scores_mm"), sem("av_mm")
        z1_mm, cen2_mm, g_mm, var2_mm = sem("z1_mm"), sem("cen2_mm"), sem("g_mm"), sem("var2_mm")
        rstd2_mm, a_mm, out_mm = sem("rstd2_mm"), sem("a_mm"), sem("out_mm")
        raw_out, scoresT_out, z_out, z1_out = sem("raw_out"), sem("scoresT_out"), sem("z_out"), sem("z1_out")
        sq2_out, cen2_out, exp_out, gelu_out = sem("sq2_out"), sem("cen2_out"), sem("exp_out"), sem("gelu_out")
        stats_done, tiny_done, smax_done, shift_done = sem("stats_done"), sem("tiny_done"), sem("smax_done"), sem("shift_done")
        den_done, rden_done, qkv_done, p1_dve = sem("den_done"), sem("rden_done"), sem("qkv_done"), sem("p1_dve")
        p2_dve, tn2_done, gated_done, x_done = sem("p2_dve"), sem("tn2_done"), sem("gated_done"), sem("x_done")
        var2_done = sem("var2_done")
        rstd1_done, rstd2_done, attn_done = sem("rstd1_done"), sem("rstd2_done"), sem("attn_done")
        p1_pool, p2_pool = sem("p1_pool"), sem("p2_pool")

        ident, center = top["consts"][:, K_ID:K_ID + P], top["consts"][:, K_CEN:K_CEN + P]
        cmean = top["consts"][:, K_MEAN:K_MEAN + P]
        cols = top["cols"]
        ND, NP = B - POOL_I, POOL_I
        x_flat = d["x"].rearrange("b c h w -> c b (h w)")
        x_rows = d["x"].rearrange("b c h w -> c b h w")
        xs = top["xs"]

        def upto(n):
            return min(n, TILES) if isinstance(n, int) else n

        def p1_product(eng, k, i):
            v = qkv[k]
            q = v[:, i, 0:C].rearrange("p (e h) -> p e h", h=HEADS).unsqueeze(2).broadcast_to([P, HD, B, HEADS])
            kk = v[:, :, C:2 * C].rearrange("p j (e h) -> p e j h", h=HEADS)
            out = prod1[:, :, C * i:C * (i + 1)].rearrange("p e (j h) -> p e j h", h=HEADS)
            return eng.tensor_tensor(out, q, kk, ALU.mult)

        def p2_product(eng, k, j):
            a = attn[:, :].rearrange("p (i j h) -> p j i h", i=B, j=B)[:, j].unsqueeze(3).broadcast_to([P, B, HEADS, HD])
            v = qkv[k][:, j, 2 * C:3 * C].rearrange("p (h e) -> p h e", h=HEADS).unsqueeze(1).broadcast_to([P, B, HEADS, HD])
            out = prod2[:, j, :].rearrange("p (i h e) -> p i h e", i=B, h=HEADS)
            return eng.tensor_tensor(out, a, v, ALU.mult)

        def pe_qkv(pe, t, k, g):
            if g == 0:
                pe.wait_ge(xt_in[k], 16 * ((t - k) // 2 + 1) if isinstance(t, int) else (t - k) * 8 + 16)
            wait(pe, raw_out, 4 * t + g - 1)
            for e in range(2):
                m = pe.matmul(q_ps[g % 2][:, e, :], top["xt"][k][:, 2 * g + e, :], top["wcat"][:, 2 * g + e, :],
                              start=True, stop=True)
            m.then_inc(qkv_mm, 1)

        def pe_scores_t(pe, t):
            wait(pe, p1_dve, ND * (t + 1))
            wait(pe, p1_pool, NP * (t + 1))
            wait(pe, tn2_done, t - 2)
            for blk in range(4):
                for e in range(HD):
                    m = pe.matmul(b2[:, P * blk:P * (blk + 1)], prod1[:, e, P * blk:P * (blk + 1)], ident,
                                  start=(e == 0), stop=(e == HD - 1), is_transpose=True)
            m.then_inc(scoresT_mm, 1)

        def pe_scores(pe, t):
            wait(pe, scoresT_out, t + 1)
            wait(pe, shift_done, t)
            wait(pe, gelu_out, 2 * (t - 1))
            for blk in range(4):
                m = pe.transpose(b3[:, P * blk:P * (blk + 1)], scoresT[:, blk, :], ident)
            m.then_inc(scores_mm, 1)

        def pe_av(pe, t):
            wait(pe, p2_dve, ND * (t + 1))
            wait(pe, p2_pool, NP * (t + 1))
            wait(pe, gated_done, 2 * t - 1)
            for p in range(PAIRS):
                if p == PAIRS - 1:
                    wait(pe, x_done, 4 * (t - 1))
                for j in range(B):
                    m = pe.matmul(b4[:, TILE * p:TILE * (p + 1)], prod2[:, j, P * p:P * (p + 1)], ident,
                                  start=(j == 0), stop=(j == B - 1), is_transpose=True)
            m.then_inc(av_mm, 1)

        def pe_z1(pe, t):
            wait(pe, z_out, t + 1)
            wait(pe, gated_done, 2 * t)
            wait(pe, tkeep_out, t + 1)
            pe.matmul(b6[:, :], top["woutT"][:, :], z[:, :], start=True, stop=False)
            for p in range(PAIRS):
                m = pe.matmul(b6[:, TILE * p:TILE * (p + 1)], tkeep[:, 2 * p:2 * p + 2, :], ident,
                              start=False, stop=(p == PAIRS - 1), is_transpose=True)
            m.then_inc(z1_mm, 1)

        traw = [sb(f"traw{k}", [P, B, C]) for k in range(2)]
        tkeep = sb("tkeep", [P, B, C])
        tkeep_out = sem("tkeep_out")

        def pe_center(pe, t, k):
            wait(pe, z1_out, t + 1)
            pe.matmul(b4[:, :], center, z1[k][:, :], start=True, stop=True).then_inc(cen2_mm, 1)

        def pe_g(pe, t, k, e):
            if e == 1:
                wait(pe, shift_done, upto(t + 2))
            half = slice(C * e, C * e + C)
            pe.matmul((b6, b3)[e][:, :], top["w2T"][half, :], z1[k][half, :], start=True, stop=True).then_inc(g_mm, 1)

        def pe_var2(pe, t):
            wait(pe, sq2_out, t + 1)
            wait(pe, cen2_out, t + 1)
            for p in range(PAIRS):
                m = pe.matmul(b4[:, P * p:P * (p + 1)], sq2[:, TILE * p:TILE * (p + 1)], cmean, start=True, stop=True)
            m.then_inc(var2_mm, 1)

        def pe_rstd2(pe, t):
            wait(pe, rrep_done, t + 1)
            wait(pe, scoresT_out, upto(t + 3))
            for p in range(PAIRS):
                m = pe.transpose(b2[:, TILE * p:TILE * (p + 1)],
                                 rrep[:, 2 * p:2 * p + 2, :].rearrange("p a b -> p (a b)"), ident)
            m.then_inc(rstd2_mm, 1)

        rrep = sb("rrep", [P, B, C])
        rrep_done = sem("rrep_done")

        def pe_a(pe, t, e):
            if e == 0:
                wait(pe, tn2_done, t + 1)
                wait(pe, var2_done, t + 1)
            else:
                wait(pe, gelu_out, 2 * t + 1)
            half = slice(C * e, C * e + C)
            pe.matmul((b4, b6)[e][:, :], top["w1T"][half, :], tn2[half, :], start=True, stop=True).then_inc(a_mm, 1)

        def rows(ap, r):
            return ap.rearrange("p (q r w) -> p r q w", q=PAIRS, r=2)[:, r]

        def out_of(e, r):
            return (b5, b7)[e][C * (1 - r):C * (1 - r) + C, 0:PAIRS * HW]

        def pe_cow(pe, t, k, e):
            if isinstance(t, int):
                wait(pe, x_done, 4 * t)
            half = slice(C * e, C * e + C)
            for r in range(2):
                pe.matmul(out_of(e, r), top["cowT"][half, :], rows(z1[k][half, :], r), start=True, stop=False)

        def pe_out(pe, t, e):
            wait(pe, gated_done, 2 * t + e + 1)
            for r in range(2):
                m = pe.matmul(out_of(e, r), top["w3T"][:, :], rows(gated[e][:, :], r), start=False, stop=True)
            m.then_inc(out_mm, 1)

        def act_raw(act, t, k, g):
            wait(act, qkv_mm, 4 * t + g + 1)
            if g == 0:
                wait(act, tkeep_out, t - 1)
                wait(act, stats_done, B * (t - 1))
                wait(act, qkv_done, B * (t - 1))
            act.activation(traw[k][:, 2 * g:2 * g + 2, :], q_ps[g % 2][:, :, 0:C], ACT.Identity)
            act.activation(raw[k][:, 2 * g:2 * g + 2, C:4 * C], q_ps[g % 2][:, :, C:4 * C], ACT.Identity)\
                .then_inc(raw_out, 1)

        def act_scores_t(act, t):
            wait(act, scoresT_mm, t + 1)
            wait(act, scores_mm, t)
            act.activation(scoresT[:, :, :].rearrange("p a b -> p (a b)"), b2[:, :], ACT.Identity).then_inc(scoresT_out, 1)

        def act_keep(act, t, k):
            wait(act, raw_out, 4 * (t + 1))
            wait(act, z1_mm, t)
            act.activation(tkeep[:, :, :], traw[k][:, :, :], ACT.Identity).then_inc(tkeep_out, 1)

        def act_z(act, t):
            wait(act, av_mm, t + 1)
            wait(act, z1_mm, t)
            act.activation(z[:, :], b4[:, :], ACT.Identity).then_inc(z_out, 1)

        def act_z1(act, t, k):
            wait(act, z1_mm, t + 1)
            act.activation(z1[k][:, :], b6[:, :], ACT.Identity, bias=cols[:, 1:2]).then_inc(z1_out, 1)

        def act_center(act, t):
            wait(act, cen2_mm, t + 1)
            wait(act, var2_mm, t)
            wait(act, tn2_done, t)
            act.activation(sq2[:, :], b4[:, :], ACT.Square).then_inc(sq2_out, 1)
            act.activation(cen2[:, :], b4[:, :], ACT.Identity).then_inc(cen2_out, 1)

        def act_exp(act, t):
            wait(act, shift_done, t + 1)
            wait(act, attn_done, t)
            wait(act, den_done, t)
            act.activation(exps[:, :], shifted[:, :], ACT.Exp, scale=float(HD) ** -0.5).then_inc(exp_out, 1)

        def act_gelu(act, t, e):
            wait(act, g_mm, 2 * t + e + 1)
            wait(act, gated_done, 2 * t + e - 1)
            act.activation(gel[e][:, :], (b6, b3)[e][:, :], ACT.Gelu, bias=cols[:, 3:4]).then_inc(gelu_out, 1)

        def dve_softmax_max(dve, t):
            wait(dve, scores_mm, t + 1)
            wait(dve, shift_done, t)
            view = b3[:, :].rearrange("p (i j h) -> p i h j", i=B, j=B)
            dve.tensor_reduce(smax[:, :].rearrange("p (i h) -> p i h", i=B), view, AX.X, ALU.max).then_inc(smax_done, 1)
            wait(dve, smax_done, t + 1)
            wait(dve, exp_out, t)
            top_of = smax[:, :].rearrange("p (i h) -> p i h", i=B).unsqueeze(2).broadcast_to([P, B, B, HEADS])
            dve.tensor_tensor(shifted[:, :].rearrange("p (i j h) -> p i j h", i=B, j=B),
                              b3[:, :].rearrange("p (i j h) -> p i j h", i=B, j=B), top_of, ALU.subtract)\
                .then_inc(shift_done, 1)

        def dve_softmax_sum(dve, t):
            wait(dve, exp_out, t + 1)
            wait(dve, rden_done, t)
            dve.tensor_reduce(den[:, :].rearrange("p (i h) -> p i h", i=B),
                              exps[:, :].rearrange("p (i j h) -> p i h j", i=B, j=B), AX.X, ALU.add).then_inc(den_done, 1)
            wait(dve, den_done, t + 1)
            wait(dve, attn_done, t)
            dve.reciprocal(rden[:, :], den[:, :]).then_inc(rden_done, 1)

        def dve_stats(dve, t, k, g):
            wait(dve, raw_out, 4 * t + g + 1)
            if g == 0:
                wait(dve, tiny_done, 5 * t)
            for i in (2 * g, 2 * g + 1):
                dve.bn_stats(st1[:, i, :], traw[k][:, i, :]).then_inc(stats_done, 1)

        def dve_var1(dve, t):
            wait(dve, stats_done, B * (t + 1))
            wait(dve, rstd1_done, t)
            dve.tensor_tensor(tiny[:, 0, :], st1[:, :, 1], st1[:, :, 4], ALU.subtract).then_inc(tiny_done, 1)
            dve.tensor_tensor(tiny[:, 1, :], st1[:, :, 2], st1[:, :, 5], ALU.add).then_inc(tiny_done, 1)
            wait(dve, tiny_done, 5 * t + 2)
            dve.scalar_tensor_tensor(tiny[:, 2, :], tiny[:, 0, :], C / 4.0, tiny[:, 0, :], ALU.mult, ALU.mult)\
                .then_inc(tiny_done, 1)
            wait(dve, tiny_done, 5 * t + 3)
            dve.tensor_tensor(tiny[:, 2, :], tiny[:, 2, :], tiny[:, 1, :], ALU.add).then_inc(tiny_done, 1)
            wait(dve, tiny_done, 5 * t + 4)
            dve.tensor_scalar(tiny[:, 3, :], tiny[:, 2, :], 1.0 / C, 1e-5, ALU.mult, ALU.add).then_inc(tiny_done, 1)

        def dve_qkv(dve, t, k):
            wait(dve, rstd1_done, t + 1)
            wait(dve, p2_pool, NP * (t - 1))
            wait(dve, p2_dve, ND * (t - 1))
            for i in range(B):
                dve.scalar_tensor_tensor(qkv[k][:, i, :], raw[k][:, i, C:4 * C], rstd1[:, i:i + 1], top["brep"][:, :],
                                         ALU.mult, ALU.add).then_inc(qkv_done, 1)

        def dve_p1(dve, t, k, images):
            wait(dve, qkv_done, B * (t + 1))
            wait(dve, scoresT_mm, t)
            for i in images:
                p1_product(dve, k, i).then_inc(p1_dve, 1)

        def dve_rrep(dve, t):
            wait(dve, rstd2_done, t + 1)
            wait(dve, rstd2_mm, t)
            dve.tensor_scalar(rrep[:, :, :], rstd2[:, :].unsqueeze(2).broadcast_to([P, B, C]), 1.0, None, ALU.mult)\
                .then_inc(rrep_done, 1)

        def dve_p2(dve, t, k, js):
            wait(dve, attn_done, t + 1)
            wait(dve, av_mm, t)
            for j in js:
                p2_product(dve, k, j).then_inc(p2_dve, 1)

        def dve_var2(dve, t):
            wait(dve, var2_mm, t + 1)
            wait(dve, rstd2_done, t)
            dve.tensor_scalar(var2[:, :], b4[:, ::C], 1e-5, None, ALU.add).then_inc(var2_done, 1)

        def dve_tn2(dve, t):
            wait(dve, rstd2_mm, t + 1)
            wait(dve, cen2_out, t + 1)
            wait(dve, a_mm, 2 * t)
            dve.tensor_tensor(tn2[:, :], b2[:, :], cen2[:, :], ALU.mult).then_inc(tn2_done, 1)

        def dve_gated(dve, t, e):
            wait(dve, a_mm, 2 * t + e + 1)
            wait(dve, gelu_out, 2 * t + e + 1)
            wait(dve, out_mm, 2 * t + e - 1)
            dve.scalar_tensor_tensor(gated[e][:, :], (b4, b6)[e][:, :], cols[:, 2:3], gel[e][:, :], ALU.add, ALU.mult)\
                .then_inc(gated_done, 1)

        def dve_x(dve, t, k):
            if isinstance(t, int):
                dve.wait_ge(xr_in[k], 32 * ((t - k) // 2 + 1))
            else:
                dve.wait_ge(xr_in[k], (t - k) * 16 + 32)
            for e in range(2):
                wait(dve, out_mm, 2 * t + e + 1)
                for r in range(2):
                    half = slice(C * (1 - r), C * (1 - r) + C)
                    dve.scalar_tensor_tensor(
                        xs[half, e::2, bass.ds(t + r, 1), :].rearrange("p q s w -> p q (s w)"),
                        out_of(e, r).rearrange("p (q w) -> p q w", q=PAIRS), cols[half, 4:5], xr[k][half, e::2, :],
                        ALU.add, ALU.add).then_inc(x_done, 1)

        def pool_rstd1(pool, t):
            wait(pool, tiny_done, 5 * t + 5)
            wait(pool, qkv_done, B * t)
            pool.tensor_tensor(rstd1[:, :], tiny[:, 3, :], top["half"][:, :], ALU.pow).then_inc(rstd1_done, 1)

        def pool_attn(pool, t):
            wait(pool, rden_done, t + 1)
            wait(pool, p2_dve, ND * t)
            wait(pool, p2_pool, NP * t)
            r = rden[:, :].rearrange("p (i h) -> p i h", i=B).unsqueeze(2).broadcast_to([P, B, B, HEADS])
            pool.tensor_tensor(attn[:, :].rearrange("p (i j h) -> p i j h", i=B, j=B),
                               exps[:, :].rearrange("p (i j h) -> p i j h", i=B, j=B), r, ALU.mult).then_inc(attn_done, 1)

        def pool_p2(pool, t, k, js):
            wait(pool, attn_done, t + 1)
            wait(pool, av_mm, t)
            for j in js:
                p2_product(pool, k, j).then_inc(p2_pool, 1)

        def pool_rstd2(pool, t):
            wait(pool, var2_done, t + 1)
            wait(pool, rrep_done, t)
            pool.tensor_tensor(rstd2[:, :], var2[:, :], top["half"][:, :], ALU.pow).then_inc(rstd2_done, 1)

        def pool_p1(pool, t, k):
            wait(pool, qkv_done, B * (t + 1))
            wait(pool, scoresT_mm, t)
            for i in range(ND, B):
                p1_product(pool, k, i).then_inc(p1_pool, 1)

        def sp_xt(sp, t, k):
            wait(sp, qkv_mm, 4 * (t - 1))
            src = x_flat[:, :, bass.ds(t * TILE, TILE)]
            sp.dma_start(top["xt"][k][0:C, :, :], src).then_inc(xt_in[k], 16)

        def sp_xr(sp, t, k):
            wait(sp, x_done, 4 * (t - 1))
            for r in range(2):
                half = slice(C * (1 - r), C * (1 - r) + C)
                sp.dma_start(xr[k][half, :, :],
                             x_rows[:, :, bass.ds(2 * t + r, 1), :].rearrange("c b r w -> c b (r w)")).then_inc(xr_in[k], 16)

        def pe_iteration(pe, t, k, new, mid, cur, old, last):
            if mid:
                pe_scores_t(pe, t + 1)
            if new:
                pe_qkv(pe, t + 2, k, 0)
            if old:
                pe_rstd2(pe, t - 1)
            if mid:
                pe_scores(pe, t + 1)
            if new:
                pe_qkv(pe, t + 2, k, 1)
                pe_qkv(pe, t + 2, k, 2)
            if old:
                pe_a(pe, t - 1, 0)
                pe_a(pe, t - 1, 1)
            if new:
                pe_qkv(pe, t + 2, k, 3)
            if cur:
                pe_av(pe, t)
            if old:
                pe_cow(pe, t - 1, 1 - k, 0)
                pe_cow(pe, t - 1, 1 - k, 1)
            if cur:
                pe_z1(pe, t)
            if old:
                pe_out(pe, t - 1, 0)
                pe_out(pe, t - 1, 1)
            if cur:
                pe_center(pe, t, k)
                pe_g(pe, t, k, 0)
                pe_g(pe, t, k, 1)
                pe_var2(pe, t)

        def act_iteration(act, t, k, new, mid, cur, old, last):
            if cur:
                act_keep(act, t, k)
            if mid:
                act_scores_t(act, t + 1)
            if new:
                act_raw(act, t + 2, k, 0)
                act_raw(act, t + 2, k, 1)
            if mid:
                act_exp(act, t + 1)
            if new:
                act_raw(act, t + 2, k, 2)
                act_raw(act, t + 2, k, 3)
            if cur:
                act_z(act, t)
                act_z1(act, t, k)
                act_center(act, t)
                act_gelu(act, t, 0)
                act_gelu(act, t, 1)

        def dve_iteration(dve, t, k, new, mid, cur, old, last):
            if cur:
                dve_p2(dve, t, k, range(0, 2))
            if old:
                dve_rrep(dve, t - 1)
            if cur:
                dve_p2(dve, t, k, range(2, ND))
            if old:
                dve_tn2(dve, t - 1)
            if mid:
                dve_softmax_max(dve, t + 1)
            if new:
                dve_stats(dve, t + 2, k, 0)
                dve_stats(dve, t + 2, k, 1)
            if last:
                dve_x(dve, t - 2, k)
            if old:
                dve_gated(dve, t - 1, 0)
                dve_gated(dve, t - 1, 1)
            if mid:
                dve_softmax_sum(dve, t + 1)
            if new:
                dve_stats(dve, t + 2, k, 2)
                dve_stats(dve, t + 2, k, 3)
                dve_var1(dve, t + 2)
                dve_qkv(dve, t + 2, k)
                dve_p1(dve, t + 2, k, range(ND))
            if cur:
                dve_var2(dve, t)

        def pool_iteration(pool, t, k, new, mid, cur, old, last):
            if old:
                pool_rstd2(pool, t - 1)
            if cur:
                pool_p2(pool, t, k, range(ND, B))
            if mid:
                pool_attn(pool, t + 1)
            if new:
                pool_rstd1(pool, t + 2)
                pool_p1(pool, t + 2, k)

        def sp_iteration(sp, t, k, new, mid, cur, old, last):
            if not isinstance(t, int) or t + 4 < TILES:
                sp_xt(sp, t + 4, k)
            if cur:
                sp_xr(sp, t, k)

        def run(eng, iteration):
            def peeled(t):
                exists = [0 <= u < TILES for u in (t + 2, t + 1, t, t - 1, t - 2)]
                iteration(eng, t, t % 2, *exists)

            first, last = 4, TILES - 4
            for t in range(-2, first):
                peeled(t)
            with eng.Fori(first // 2, last // 2) as pair:
                for k in range(2):
                    iteration(eng, pair * 2 + k, k, True, True, True, True, True)
            for t in range(last, TILES + 2):
                peeled(t)

        block = ctx.enter_context(nc.Block())

        @block.tensor
        def _(pe):
            run(pe, pe_iteration)

        @block.scalar
        def _(act):
            run(act, act_iteration)

        @block.vector
        def _(dve):
            run(dve, dve_iteration)

        @block.gpsimd
        def _(pool):
            run(pool, pool_iteration)

        @block.sync
        def _(sp):
            sp_xt(sp, 0, 0)
            sp_xt(sp, 1, 1)
            run(sp, sp_iteration)


def conv_steps(nc, d, top):
    with ExitStack() as ctx:
        def sb(name, shape, dt=F32):
            return ctx.enter_context(nc.sbuf_tensor(name, shape, dt))

        def sem(name):
            return ctx.enter_context(nc.semaphore(name))

        xs, cols = top["xs"], top["cols"]
        a_hi, a_lo = (sb(n, [P, SLOTS, PADW], F32R) for n in ("a_hi", "a_lo"))
        m_hi, m_lo = (sb(n, [P, SLOTS + 1, PADW], F32R) for n in ("m_hi", "m_lo"))
        RING = 3
        evac = [sb(f"evac{k}", [P, 8, HW]) for k in range(RING)]
        result = sb("result", [P, SLOTS, HW])
        banks = [ctx.enter_context(nc.psum_tensor(f"conv{k}", [P, 8, HW], F32)) for k in range(8)]
        zeroed, conv_mm, evac_out, split_x, split_m = sem("zeroed"), sem("conv_mm"), sem("evac_out"), sem("split_x"), sem("split_m")
        x_added, hi_done, result_done, stored = sem("x_added"), sem("hi_done"), sem("result_done"), sem("stored")

        QA = [(8 * q, 8) for q in range(4)] + [(SLOTS - 1, 1)]
        QM = [(8 * q, 8) for q in range(4)]
        PER_STEP = len(QA) + len(QM)
        PER_IMAGE = STEPS * PER_STEP
        tiles = [(s, c, q) for s in range(STEPS) for c in range(2) for q in range(len((QM, QA)[c]))]
        NA, NM = len(QA), len(QM)

        def bank_free(n):
            before = [k for k in range(n) if k % 8 == n % 8]
            return before[-1] + 1 if before else [k for k in range(PER_IMAGE) if k % 8 == n % 8][-1] + 1 - PER_IMAGE

        def pe_image(pe, img, first):
            for n, (s, c, q) in enumerate(tiles):
                base = img * PER_IMAGE
                need = bank_free(n)
                if not (first and need <= 0):
                    pe.wait_ge(evac_out, base + need)
                if c == 0:
                    pe.wait_ge(split_x, img * (NA * STEPS) + (NA * s + q + 2))
                else:
                    pe.wait_ge(split_m, img * (NM * STEPS) + (NM * s + min(q + 1, NM)))
                s0, cnt = (QM, QA)[c][q]
                hi, lo = ((a_hi, a_lo), (m_hi, m_lo))[c]
                wh, wl = top["cwh"][c], top["cwl"][c]
                k = 0
                for slot in range(2):
                    for kx in range(TAPS):
                        for w, v in ((wh, hi), (wh, lo), (wl, hi)):
                            m = pe.matmul(banks[n % 8][:, 0:cnt, :], w[:, slot, kx, :],
                                          v[:, s0 + slot:s0 + slot + cnt, kx:kx + HW],
                                          start=(k == 0), stop=(k == 6 * TAPS - 1))
                            k += 1
                m.then_inc(conv_mm, 1)

        def act_image(act, img, first):
            for n, (s, c, q) in enumerate(tiles):
                act.wait_ge(conv_mm, img * PER_IMAGE + n + 1)
                s0, cnt = (QM, QA)[c][q]
                if not (first and n < RING):
                    act.wait_ge(*freed(img, n))
                if c == 0:
                    act.activation(evac[n % RING][:, 0:cnt, :], banks[n % 8][:, 0:cnt, :], ACT.Relu,
                                   bias=cols[:, 6:7]).then_inc(evac_out, 1)
                else:
                    act.activation(evac[n % RING][:, 0:cnt, :], banks[n % 8][:, 0:cnt, :], ACT.Identity,
                                   bias=cols[:, 8:9], scale=H_STEP).then_inc(evac_out, 1)

        def freed(img, n):
            k = n - RING
            back = 0 if k >= 0 else 1
            s, c, q = tiles[k % PER_IMAGE]
            if c == 0:
                return split_m, (img * (NM * STEPS)) + (NM * s + q + 1 - back * NM * STEPS)
            return x_added, (img * (XA * STEPS)) + (XA * s + adds(q + 1) - back * XA * STEPS)

        XA = NA + 1

        def adds(q):
            return q + 1 if q else 0

        def split(dve, src, hi, lo, img, count, what):
            dve.tensor_scalar(hi, src, 1.0, None, ALU.mult).then_inc(hi_done, 1)
            dve.wait_ge(hi_done, count)
            dve.tensor_tensor(lo, src, hi.bitcast(F32), ALU.subtract).then_inc(what, 1)

        HI = (NA + NM) * STEPS

        def x_of(img, s0, cnt):
            return xs[:, bass.ds(img, 1), s0:s0 + cnt, :].rearrange("p b s w -> p (b s) w")

        def first_split(dve, img, n0):
            for q, (s0, cnt) in enumerate(QA):
                split(dve, x_of(img, s0, cnt), a_hi[:, s0:s0 + cnt, 1:1 + HW], a_lo[:, s0:s0 + cnt, 1:1 + HW],
                      img, img * HI + (n0 + q + 1), split_x)

        def dve_image(dve, img, last):
            h = NA
            x_adds = 0
            for n, (s, c, q) in enumerate(tiles):
                s0, cnt = (QM, QA)[c][q]
                dve.wait_ge(evac_out, img * PER_IMAGE + n + 1)
                src = evac[n % RING][:, 0:cnt, :]
                if c == 0:
                    h += 1
                    split(dve, src, m_hi[:, s0 + 1:s0 + 1 + cnt, 1:1 + HW], m_lo[:, s0 + 1:s0 + 1 + cnt, 1:1 + HW],
                          img, img * HI + h, split_m)
                    if s == STEPS - 1 and q == NM - 1 and not last:
                        first_split(dve, img + 1, 0)
                    continue
                parts = [(slice(0, P), s0, cnt)]
                if q == 0:
                    parts = [(slice(C, P), 0, 1), (slice(0, P), 1, cnt - 1)]
                if q == NA - 1:
                    parts = [(slice(0, C), s0, 1)]
                for part, p0, pc in parts:
                    x_adds += 1
                    xv = xs[part, bass.ds(img, 1), p0:p0 + pc, :].rearrange("p b s w -> p (b s) w")
                    dve.tensor_tensor(xv, xv, evac[n % RING][part, p0 - s0:p0 - s0 + pc, :], ALU.add).then_inc(x_added, 1)
                dve.wait_ge(x_added, img * (XA * STEPS) + x_adds)
                if s < STEPS - 1:
                    h += 1
                    split(dve, x_of(img, s0, cnt), a_hi[:, s0:s0 + cnt, 1:1 + HW], a_lo[:, s0:s0 + cnt, 1:1 + HW],
                          img, img * HI + h, split_x)
                else:
                    if q == 0 and not (isinstance(img, int) and img == 0):
                        dve.wait_ge(stored, img * STORED)
                    dve.tensor_scalar(result[:, s0:s0 + cnt, :], x_of(img, s0, cnt), 0.0, None, ALU.max)\
                        .then_inc(result_done, 1)

        out = d["out"].rearrange("b c (p r) w -> b r c p w", r=2)
        STORED = 16 * 2 * NM

        def sp_image(sp, img):
            for q in range(NM):
                sp.wait_ge(result_done, img * NA + q + 2)
                s0 = 8 * q
                sp.dma_start(out[bass.ds(img, 1), 0, :, s0:s0 + 8, :].rearrange("b c p w -> (b c) p w"),
                             result[C:P, s0:s0 + 8, :]).then_inc(stored, 16)
                sp.dma_start(out[bass.ds(img, 1), 1, :, s0:s0 + 8, :].rearrange("b c p w -> (b c) p w"),
                             result[0:C, s0 + 1:s0 + 9, :]).then_inc(stored, 16)

        block = ctx.enter_context(nc.Block())

        @block.tensor
        def _(pe):
            pe.wait_ge(zeroed, 6)
            pe_image(pe, 0, True)
            with pe.Fori(1, B) as img:
                pe_image(pe, img, False)

        @block.scalar
        def _(act):
            act_image(act, 0, True)
            with act.Fori(1, B) as img:
                act_image(act, img, False)

        @block.vector
        def _(dve):
            for t in (a_hi, a_lo, m_hi, m_lo):
                dve.memset(t[:, :, :].bitcast(F32), 0.0).then_inc(zeroed, 1)
            dve.memset(xs[0:C, :, 0, :], 0.0).then_inc(zeroed, 1)
            dve.memset(xs[C:P, :, SLOTS - 1, :], 0.0).then_inc(zeroed, 1)
            dve.wait_ge(zeroed, 6)
            first_split(dve, 0, 0)
            dve_image(dve, 0, False)
            with dve.Fori(1, B - 1) as img:
                dve_image(dve, img, False)
            dve_image(dve, B - 1, True)

        @block.sync
        def _(sp):
            with sp.Fori(0, B) as img:
                sp_image(sp, img)
            sp.wait_ge(stored, STORED * B)


def program(nc, d):
    with ExitStack() as ctx:
        def sb(name, shape, dt=F32):
            return ctx.enter_context(nc.sbuf_tensor(name, shape, dt))

        top = {
            "consts": sb("consts", [P, K_END]),
            "cols": sb("cols", [P, 9]),
            "half": sb("half", [P, B]),
            "xt": [sb(f"xt{k}", [C + 1, B, TILE]) for k in range(2)],
            "wcat": sb("wcat", [C + 1, B, 4 * C]),
            "woutT": sb("woutT", [P, P]), "cowT": sb("cowT", [P, C]),
            "w1T": sb("w1T", [P, HID]), "w2T": sb("w2T", [P, HID]), "w3T": sb("w3T", [HID, C]),
            "brep": sb("brep", [P, 3 * C]),
            "cwh": [sb(f"cwh{k}", [P, 2, TAPS, P], F32R) for k in range(2)],
            "cwl": [sb(f"cwl{k}", [P, 2, TAPS, P], F32R) for k in range(2)],
            "xs": sb("xs", [P, B, SLOTS, HW]),
        }
        setup_weights(nc, d, None, top)
        attention_block(nc, d, top)
        conv_steps(nc, d, top)


_INS = ["x"] + ["L0_conv_" + n for n in (
    "gn_g gn_b ciw cib pe ln1g ln1b wq bq wk bk wv bv win bin_ wout bout ln2g ln2b w1 b1 w2 b2 w3 b3 cow cob").split()] \
    + ["L1_conv_" + n for n in "w1 b1 w2 b2".split()]


def kernel(**inputs):
    import numpy as np
    import concourse.bacc as bacc
    from concourse import mybir as mb
    from concourse.bass_utils import run_bass_kernel_spmd

    consts = np.zeros((P, K_END), np.float32)
    consts[:, K_ID:K_ID + P] = np.eye(P)
    for k in range(2):
        half = slice(C * k, C * k + C)
        consts[half, K_CEN + C * k:K_CEN + C * k + C] = np.eye(C) - 1.0 / C
        consts[half, K_MEAN + C * k:K_MEAN + C * k + C] = 1.0 / C
    for g in range(P // 8):
        consts[8 * g:8 * g + 8, K_GRP + 8 * g:K_GRP + 8 * g + 8] = 1.0 / 8

    nc = bacc.Bacc("TRN2", target_bir_lowering=False, num_devices=1)
    arrays, d = {}, {}
    for name in _INS:
        a = np.ascontiguousarray(inputs[name])
        arrays[f"in_{name}"] = a
        d[name] = nc.dram_tensor(f"in_{name}", a.shape, mb.dt.from_np(a.dtype), kind="ExternalInput").ap()
    arrays["in_consts"] = consts
    d["consts"] = nc.dram_tensor("in_consts", consts.shape, mb.dt.float32, kind="ExternalInput").ap()
    d["out"] = nc.dram_tensor("out_y", (B, C, HW, HW), mb.dt.float32, kind="ExternalOutput").ap()
    program(nc, d)
    r = run_bass_kernel_spmd(nc, [arrays], core_ids=[0])
    return r.results[0]["out_y"]
```

```python
import concourse.bass as bass
from concourse import mybir
from contextlib import ExitStack

B, C, HW = 8, 64, 64
HEADS = 8
HD = C // HEADS
HID = 2 * C
PIX = HW * HW
TILE = 2 * HW
TILES = PIX // TILE
PAIRS = B // 2
P = 2 * C
SLOTS = HW // 2 + 1
PADW = HW + 2
STEPS = 3
H_STEP = 1.0 / 3.0
TAPS = 3
PRODS = 4
DUO = HW // 2
POOL_I = 3
F32, F32R = mybir.dt.float32, mybir.dt.float32r
ALU, ACT, AX = mybir.AluOpType, mybir.ActivationFunctionType, mybir.AxisListType
K_ID, K_CEN, K_MEAN, K_GRP, K_END = 0, P, 2 * P, 3 * P, 4 * P


def wait(eng, sem, n):
    if isinstance(n, int) and n <= 0:
        return
    eng.wait_ge(sem, n)


def setup_weights(nc, d, top):
    with ExitStack() as ctx:
        def sb(name, shape, dt=F32):
            return ctx.enter_context(nc.sbuf_tensor(name, shape, dt))

        def ps(name, shape):
            return ctx.enter_context(nc.psum_tensor(name, shape, F32))

        def sem(name):
            return ctx.enter_context(nc.semaphore(name))

        win = sb("win", [C, 3, C])
        wqkv = sb("wqkv", [C, 3, C])
        ciw = sb("ciw", [C, C])
        wout2 = sb("wout2", [C, 2, C])
        cow2 = sb("cow2", [C, 2, C])
        w1n = sb("w1n", [HID, 2, C])
        w2n = sb("w2n", [HID, 2, C])
        w3n = sb("w3n", [C, HID])
        binr = sb("binr", [1, 3 * C])
        ones1 = sb("ones1", [1, P])
        vec = sb("vec", [C, 12])
        pen = sb("pen", [B, C])
        pet = sb("pet", [C, B])
        cw = [sb(f"cw{k}", [C, C, TAPS * TAPS]) for k in range(2)]
        cw2 = sb("cw2", [C, TAPS * TAPS, 2, C])
        wiT = sb("wiT", [C, 3, C])
        rq = sb("rq", [C, 3 * C])
        rqg = sb("rqg", [C, 3 * C])
        basis = sb("basis", [C, 4 * C])
        reps = sb("reps", [C, 4, P])
        w1raw = sb("w1raw", [P, HID])
        wall = sb("wall", [C, 4 * C])
        cowrep = sb("cowrep", [C, 2, C])
        convf = sb("convf", [P, 2, TAPS, P])
        convu = sb("convu", [P, 2, PRODS, P])
        outer = sb("outer", [P, 2, P])
        xst = top["xs"][:, :, :, :].rearrange("p b s w -> p (b s w)")
        st = sb("st", [P, 8, 6])
        mv = sb("mv", [P, PAIRS, 2])
        means = sb("means", [P, PAIRS])
        dev = sb("dev", [P, PAIRS])
        wvar = sb("wvar", [P, PAIRS])
        mu = sb("mu", [C, B])
        gvar = sb("gvar", [C, B])
        gexp = sb("gexp", [C, B])
        ga = sb("ga", [C, B])
        gb = sb("gb", [C, B])
        cvec = sb("cvec", [C, B])
        beta = sb("beta", [B, 2, 4 * C], F32R)
        pt = [ps(f"pset{k}", [P, 512]) for k in range(8)]

        core_loaded, rest_loaded, pe_done, dve_done = sem("core_loaded"), sem("rest_loaded"), sem("pe_done"), sem("dve_done")
        taps_loaded, cw2_done, taps_mm, convf_zero = sem("taps_loaded"), sem("cw2_done"), sem("taps_mm"), sem("convf_zero")
        convf_out, outer_done, sides_done, scaled = sem("convf_out"), sem("outer_done"), sem("sides_done"), sem("scaled")
        whi_done, wlo_done, wcat_act = sem("whi_done"), sem("wlo_done"), sem("wcat_act")
        xin = [sem(f"xin{p}") for p in range(PAIRS)]
        rs_ready, beta_moved = sem("rs_ready"), sem("beta_moved")
        GN_G, GN_B, LN1G, LN1B, BQ, BK, BV, CIB, B3, LN2B = range(10)
        ident, center = top["consts"][:, K_ID:K_ID + P], top["consts"][:, K_CEN:K_CEN + P]
        group = sb("group", [P, P])

        def twice(name):
            rows, width = d[name].shape
            return d[name].unsqueeze(1).broadcast_to([rows, 2, width])

        def column(name):
            return d[name].rearrange("(n a) -> n a", a=1)

        core = [
            (win[:, :, :], d["L0_conv_win"].rearrange("(t o) i -> o t i", t=3)),
            (top["consts"][:, :], d["consts"][:, 0:K_GRP]), (group[:, :], d["consts"][:, K_GRP:K_END]),
            (wout2[:, :, :], twice("L0_conv_wout")), (cow2[:, :, :], twice("L0_conv_cow")),
            (pen[:, :], d["L0_conv_pe"][0:B, :]),
            (wqkv[:, 0, :], d["L0_conv_wq"]), (wqkv[:, 1, :], d["L0_conv_wk"]), (wqkv[:, 2, :], d["L0_conv_wv"]),
            (w1n[:, :, :], twice("L0_conv_w1")), (w2n[:, :, :], twice("L0_conv_w2")),
            (ciw[:, :], d["L0_conv_ciw"]), (binr[:, :], d["L0_conv_bin_"].rearrange("(a n) -> a n", a=1)),
        ]
        core += [(vec[:, col:col + 1], column(name)) for col, name in
                 ((LN1G, "L0_conv_ln1g"), (LN1B, "L0_conv_ln1b"), (BQ, "L0_conv_bq"), (BK, "L0_conv_bk"),
                  (BV, "L0_conv_bv"))]
        rest = [(top["cols"][C * k:C * k + C, 0:1], column("L0_conv_ln2g")) for k in range(2)]
        rest += [(w3n[:, :], d["L0_conv_w3"])]
        rest += [(vec[:, col:col + 1], column(name)) for col, name in
                 ((B3, "L0_conv_b3"), (LN2B, "L0_conv_ln2b"), (GN_G, "L0_conv_gn_g"), (GN_B, "L0_conv_gn_b"),
                  (CIB, "L0_conv_cib"))]
        rest += [(top["cols"][:, col:col + 1], column(name)) for col, name in ((2, "L0_conv_b1"), (3, "L0_conv_b2"))]
        rest += [(top["cols"][C * k:C * k + C, col:col + 1], column(name)) for k in range(2) for col, name in
                 ((1, "L0_conv_bout"), (4, "L0_conv_cob"), (6, "L1_conv_b1"), (7, "L1_conv_b2"))]
        taps = [(cw[k][:, :, :], d[f"L1_conv_w{k + 1}"].rearrange("o i a b -> o i (a b)")) for k in range(2)]
        all_core, all_rest = 16 * len(core), 16 * len(rest)
        at = {}

        block = ctx.enter_context(nc.Block())

        def x_pair(p):
            return d["x"][2 * p:2 * p + 2].rearrange("b c h w -> (b c) (h w)")

        blocks = [(ky, a, b, slot) for ky in range(TAPS) for a in range(2) for b in range(2) for slot in range(2)
                  if 2 * slot + a - b == ky]
        BLOCKS = len(blocks)

        def conv_weights_act(act, k):
            h = (1.0, H_STEP)[k]
            wait(act, taps_mm, k)
            for half in range(2):
                act.activation(cw2[:, :, half, :], cw[k][:, :, :].rearrange("o i t -> o t i"), ACT.Identity)\
                    .then_inc(cw2_done, 1)
            act.wait_ge(taps_mm, k + 1)
            act.wait_ge(convf_zero, k + 1)
            for ky, a, b, slot in blocks:
                ra, rb = slice(C * a, C * a + C), slice(C * b, C * b + C)
                act.activation(convf[ra, slot, :, rb], pt[3 + ky][ra, 0:TAPS * C].rearrange("p (t o) -> p t o", t=TAPS),
                               ACT.Identity).then_inc(convf_out, 1)
            act.wait_ge(convf_out, BLOCKS * (k + 1))
            wait(act, wlo_done, k)
            act.activation(convu[:, :, 0, :], convf[:, :, 0, :], ACT.Identity, scale=h).then_inc(scaled, 1)
            act.activation(convu[:, :, 1, :], convf[:, :, 2, :], ACT.Identity, scale=-h).then_inc(scaled, 1)
            act.wait_ge(sides_done, 2 * (k + 1))
            act.activation(convu[:, :, 2:4, :], convu[:, :, 2:4, :], ACT.Identity, scale=0.5 * h).then_inc(scaled, 1)
            act.wait_ge(scaled, 3 * (k + 1))
            act.activation(top["cwh"][k][:, :, :, :], convu[:, :, :, :], ACT.Identity).then_inc(whi_done, 1)

        def conv_weights_pool(pool, k):
            wait(pool, scaled, 3 * k)
            wait(pool, sides_done, 2 * k)
            wait(pool, wlo_done, k)
            pool.memset(convf[:, :, :, :], 0.0).then_inc(convf_zero, 1)
            pool.wait_ge(convf_out, BLOCKS * (k + 1))
            pool.tensor_tensor(outer[:, :, :], convf[:, :, 0, :], convf[:, :, 2, :], ALU.add).then_inc(outer_done, 1)
            pool.wait_ge(outer_done, k + 1)
            for j, op in ((2, ALU.add), (3, ALU.subtract)):
                pool.tensor_tensor(convu[:, :, j, :], outer[:, :, :], convf[:, :, 1, :], op).then_inc(sides_done, 1)
            pool.wait_ge(whi_done, k + 1)
            pool.tensor_tensor(top["cwl"][k][:, :, :, :], convu[:, :, :, :], top["cwh"][k][:, :, :, :].bitcast(F32),
                               ALU.subtract).then_inc(wlo_done, 1)

        @block.vector
        def _(dve):
            n = [0]

            def link(ins, name=None):
                n[0] += 1
                ins.then_inc(dve_done, 1)
                dve.wait_ge(dve_done, n[0])
                if name:
                    at[name] = n[0]

            def gn_chunks():
                n = yield
                done = 0
                for p in range(PAIRS):
                    dve.wait_ge(xin[p], 16)
                    for q in range(8):
                        link(dve.bn_stats(st[:, q, :], xst[:, PIX * p + 512 * q:PIX * p + 512 * (q + 1)]))
                        if q == 7:
                            link(dve.bn_aggr(mv[:, p, :], st[:, :, :]))
                        done += 1
                        if done == n:
                            n, done = (yield), 0
                yield

            def low_weights(i):
                dve.wait_ge(wcat_act, i + 1)
                link(dve.scalar_tensor_tensor(top["wcat_lo"][0:C, i, :], wall[:, :], ga[:, i:i + 1],
                                              top["wcat_hi"][0:C, i, :].bitcast(F32), ALU.mult, ALU.subtract))

            link(dve.memset(ones1[:, :], 1.0))
            link(dve.memset(gexp[:, :], -0.5))
            link(dve.memset(top["half"][:, :], -0.5))
            link(dve.memset(top["xt_hi"][C:C + 1, :, :].bitcast(F32), 1.0))
            link(dve.memset(top["xt_lo"][C:C + 1, :, :].bitcast(F32), 0.0))
            link(dve.memset(top["woutT"][:, :], 0.0), "zeros")
            stats = gn_chunks()
            next(stats)
            dve.wait_ge(core_loaded, all_core)
            for k, col in enumerate((LN1B, BQ, BK, BV)):
                link(dve.tensor_copy(reps[:, k, :], vec[:, col:col + 1].broadcast_to([C, P])))
            dve.wait_ge(pe_done, 1)
            link(dve.tensor_copy(wiT[:, :, :], pt[0][0:C, 0:3 * C].rearrange("p (t o) -> p t o", t=3)), "wiT")
            dve.wait_ge(pe_done, 2)
            for k in range(2):
                half = slice(C * k, C * k + C)
                link(dve.tensor_copy(top["woutT"][half, half], pt[1][half, 0:C]))
            link(dve.tensor_copy(pet[:, :], pt[1][0:C, 2 * C:2 * C + B]))
            link(dve.tensor_copy(top["cowT"][:, :], pt[1][:, C:2 * C]))
            for k in range(2):
                link(dve.tensor_copy(cowrep[:, k, :], pt[1][0:C, C:2 * C]), "cowT")
            dve.wait_ge(pe_done, 3)
            link(dve.tensor_copy(w1raw[:, :], pt[2][:, 0:HID]))
            link(dve.tensor_copy(top["w2T"][:, :], pt[2][:, HID:2 * HID]), "w1raw")
            dve.wait_ge(pe_done, 4)
            link(dve.tensor_copy(rq[:, :], pt[3][0:C, 0:3 * C]))
            link(dve.tensor_scalar(rqg[:, :], pt[3][0:C, 0:3 * C], vec[:, LN1G:LN1G + 1], None, ALU.mult), "rq")
            dve.wait_ge(pe_done, 6)
            link(dve.tensor_copy(basis[:, 0:C], ident[0:C, 0:C]))
            for k in range(2):
                cols = slice(C * (k + 1), C * (k + 2))
                link(dve.tensor_copy(basis[:, cols].rearrange("p (e h) -> p e h", h=HEADS),
                                     pt[4][0:C, C * k:C * (k + 1)].rearrange("p (h e) -> p e h", h=HEADS)))
                link(dve.tensor_copy(top["brep"][:, C * k:C * (k + 1)].rearrange("p (e h) -> p e h", h=HEADS),
                                     pt[5][:, C * k:C * (k + 1)].rearrange("p (h e) -> p e h", h=HEADS)))
            link(dve.tensor_copy(basis[:, 3 * C:4 * C], pt[4][0:C, 2 * C:3 * C]))
            link(dve.tensor_copy(top["brep"][:, 2 * C:3 * C], pt[5][:, 2 * C:3 * C]), "basis")
            dve.wait_ge(pe_done, 7)
            link(dve.tensor_copy(wall[:, :], pt[0][0:C, 0:4 * C]), "wall")
            stats.send(16)
            dve.wait_ge(rest_loaded, all_rest)
            link(dve.tensor_scalar(top["w1T"][:, :], w1raw[:, :], top["cols"][:, 0:1], None, ALU.mult))
            dve.wait_ge(pe_done, 8)
            link(dve.tensor_copy(top["w3T"][:, :], pt[1][:, 0:C]))
            dve.wait_ge(pe_done, 9)
            link(dve.tensor_tensor(top["cols"][:, 4:5], pt[2][:, 0:1], top["cols"][:, 4:5], ALU.add))
            link(dve.tensor_tensor(top["cols"][:, 2:3], pt[2][:, 8:9], top["cols"][:, 2:3], ALU.add))
            link(dve.tensor_scalar(top["cols"][:, 8:9], top["cols"][:, 7:8], H_STEP, None, ALU.mult), "small")
            stats.send(16)
            link(dve.tensor_copy(means[:, :], mv[:, :, 0]), "means")
            dve.wait_ge(pe_done, 10)
            link(dve.tensor_tensor(dev[:, :], means[:, :], pt[6][:, 0:PAIRS], ALU.subtract))
            link(dve.tensor_tensor(dev[:, :], dev[:, :], dev[:, :], ALU.mult))
            link(dve.tensor_tensor(wvar[:, :], mv[:, :, 1], dev[:, :], ALU.add), "wvar")
            dve.wait_ge(pe_done, 11)
            link(dve.tensor_copy(mu[:, :].rearrange("c (p e) -> c e p", e=2),
                                 pt[7][0:C, 0:B].rearrange("c (e p) -> c e p", e=2)))
            link(dve.tensor_scalar(gvar[:, :].rearrange("c (p e) -> c e p", e=2),
                                   pt[7][0:C, B:2 * B].rearrange("c (e p) -> c e p", e=2), 1e-6, None, ALU.add), "gvar")
            dve.wait_ge(rs_ready, 1)
            link(dve.tensor_scalar(ga[:, :], ga[:, :], vec[:, GN_G:GN_G + 1], None, ALU.mult), "ga")
            link(dve.tensor_tensor(mu[:, :], mu[:, :], ga[:, :], ALU.mult))
            link(dve.tensor_scalar(gb[:, :], mu[:, :], -1.0, vec[:, GN_B:GN_B + 1], ALU.mult, ALU.add), "gb")
            for i in range(2):
                low_weights(i)
            dve.wait_ge(pe_done, 12)
            link(dve.scalar_tensor_tensor(cvec[:, :], pt[0][0:C, 0:B], vec[:, CIB:CIB + 1], pet[:, :],
                                          ALU.add, ALU.add), "cvec")
            for i in range(2, 4):
                low_weights(i)
            dve.wait_ge(pe_done, 13)
            link(dve.tensor_copy(beta[:, 0, :], pt[1][0:B, 0:4 * C]))
            link(dve.tensor_tensor(beta[:, 1, :], pt[1][0:B, 0:4 * C], beta[:, 0, :].bitcast(F32), ALU.subtract), "beta")
            for i in range(4, B):
                low_weights(i)

        @block.sync
        def _(sp):
            for dst, src in core[0::2]:
                sp.dma_start(dst, src).then_inc(core_loaded, 16)
            for p in range(PAIRS):
                sp.dma_start(xst[:, PIX * p:PIX * (p + 1)], x_pair(p)).then_inc(xin[p], 16)
            sp.dma_start(top["xt"][:, :, :], d["x"].rearrange("b c h w -> c b (h w)")[:, :, 0:TILE])\
                .then_inc(top["xt_in"], 16)
            sp.wait_ge(dve_done, at["beta"])
            for part, weights in enumerate((top["wcat_hi"], top["wcat_lo"])):
                sp.dma_start(weights[C:C + 1, :, :].bitcast(F32), beta[:, part, :].bitcast(F32)).then_inc(beta_moved, 16)
            sp.wait_ge(beta_moved, 32)

        @block.scalar
        def _(act):
            for dst, src in core[1::2]:
                act.dma_start(dst, src).then_inc(core_loaded, 16)
            act.wait_ge(taps_loaded, 16 * len(taps))
            for k in range(2):
                conv_weights_act(act, k)
            act.wait_ge(dve_done, at["ga"])
            for i in range(B):
                act.activation(top["wcat_hi"][0:C, i, :], wall[:, :], ACT.Identity, scale=ga[:, i:i + 1])\
                    .then_inc(wcat_act, 1)

        @block.gpsimd
        def _(pool):
            for dst, src in taps:
                pool.dma_start(dst, src).then_inc(taps_loaded, 16)
            for dst, src in rest:
                pool.dma_start(dst, src).then_inc(rest_loaded, 16)
            for k in range(2):
                conv_weights_pool(pool, k)
            pool.wait_ge(dve_done, at["gvar"])
            pool.tensor_tensor(ga[:, :], gvar[:, :], gexp[:, :], ALU.pow).then_inc(rs_ready, 1)

        @block.tensor
        def _(pe):
            def need(name):
                pe.wait_ge(dve_done, at[name])

            pe.wait_ge(core_loaded, all_core)
            for t in range(3):
                m = pe.transpose(pt[0][0:C, C * t:C * (t + 1)], win[:, t, :], ident[0:C, 0:C])
            m.then_inc(pe_done, 1)
            pe.transpose(pt[1][:, 0:C], wout2[:, :, :].rearrange("p a b -> p (a b)"), ident[0:C, 0:C])
            pe.transpose(pt[1][0:C, 2 * C:2 * C + B], pen[:, :], ident[0:B, 0:B])
            pe.transpose(pt[1][:, C:2 * C], cow2[:, :, :].rearrange("p a b -> p (a b)"),
                         ident[0:C, 0:C]).then_inc(pe_done, 1)
            pe.transpose(pt[2][:, 0:HID], w1n[:, :, :].rearrange("p a b -> p (a b)"), ident)
            pe.transpose(pt[2][:, HID:2 * HID], w2n[:, :, :].rearrange("p a b -> p (a b)"),
                         ident).then_inc(pe_done, 1)
            need("wiT")
            for t in range(3):
                m = pe.matmul(pt[3][0:C, C * t:C * (t + 1)], wqkv[:, t, :], wiT[:, t, :], start=True, stop=True)
            m.then_inc(pe_done, 1)
            need("rq")
            pe.matmul(pt[4][0:C, 0:3 * C], center[0:C, 0:C], rqg[:, :], start=True, stop=True).then_inc(pe_done, 1)
            pe.matmul(pt[5][:, 0:3 * C], reps[:, 0, :], rq[:, :], start=True, stop=False)
            for t in range(3):
                pe.matmul(pt[5][:, C * t:C * (t + 1)], reps[:, 1 + t, :], wiT[:, t, :], start=False, stop=False)
            pe.matmul(pt[5][:, 0:3 * C], ones1[:, :], binr[:, :], start=False, stop=True).then_inc(pe_done, 1)
            need("basis")
            pe.matmul(pt[0][0:C, 0:4 * C], ciw[:, :], basis[:, :], start=True, stop=True).then_inc(pe_done, 1)
            need("cowT")
            pe.wait_ge(rest_loaded, all_rest)
            pe.matmul(pt[1][:, 0:C], w3n[:, :], top["cowT"][0:C, :], start=True, stop=True).then_inc(pe_done, 1)
            need("w1raw")
            pe.matmul(pt[2][:, 0:1], cowrep[:, :, :].rearrange("p a b -> p (a b)"), vec[:, B3:B3 + 1],
                      start=True, stop=True)
            pe.matmul(pt[2][:, 8:9], w1raw[0:C, :], vec[:, LN2B:LN2B + 1], start=True, stop=True)\
                .then_inc(pe_done, 1)
            for k in range(2):
                pe.wait_ge(cw2_done, 2 * (k + 1))
                wait(pe, convf_out, BLOCKS * k)
                for ky in range(TAPS):
                    for kx in range(TAPS):
                        m = pe.transpose(pt[3 + ky][:, C * kx:C * (kx + 1)],
                                         cw2[:, TAPS * ky + kx, :, :].rearrange("p a b -> p (a b)"), ident[0:C, 0:C])
                m.then_inc(taps_mm, 1)
            need("means")
            pe.matmul(pt[6][:, 0:PAIRS], group[:, :], means[:, :], start=True, stop=True).then_inc(pe_done, 1)
            need("wvar")
            for k, src in enumerate((means, wvar)):
                for e in range(2):
                    m = pe.matmul(pt[7][0:C, B * k + PAIRS * e:B * k + PAIRS * (e + 1)], group[:, C * e:C * (e + 1)],
                                  src[:, :], start=True, stop=True)
            m.then_inc(pe_done, 1)
            need("gb")
            pe.matmul(pt[0][0:C, 0:B], wall[:, 0:C], gb[:, :], start=True, stop=True).then_inc(pe_done, 1)
            need("cvec")
            pe.matmul(pt[1][0:B, 0:4 * C], cvec[:, :], basis[:, :], start=True, stop=True).then_inc(pe_done, 1)


def attention_block(nc, d, top):
    with ExitStack() as ctx:
        def sb(name, shape, dt=F32):
            return ctx.enter_context(nc.sbuf_tensor(name, shape, dt))

        def ps(name, shape):
            return ctx.enter_context(nc.psum_tensor(name, shape, F32))

        def sem(name):
            return ctx.enter_context(nc.semaphore(name))

        N = PAIRS * TILE
        S = B * B * HEADS
        raw = [sb(f"raw{k}", [P, B, 3 * C]) for k in range(2)]
        qkv = [sb(f"qkv{k}", [P, B, 3 * C]) for k in range(2)]
        xr = [sb(f"xr{k}", [P, B, HW]) for k in range(2)]
        prod1 = sb("prod1", [P, HD, S])
        prod2 = sb("prod2", [P, B, B * C])
        st1 = sb("st1", [P, B, 6])
        tiny = sb("tiny", [P, 4, B])
        rstd1 = sb("rstd1", [P, B])
        rstd2 = sb("rstd2", [P, B])
        var2 = sb("var2", [P, B])
        scoresT = sb("scoresT", [P, 4, P])
        smax = sb("smax", [P, C])
        shifted = sb("shifted", [P, S])
        exps = shifted
        den = smax
        rden = sb("rden", [P, C])
        attn = sb("attn", [P, S])
        z = sb("z", [P, N])
        z1 = [sb(f"z1_{k}", [P, N]) for k in range(2)]
        cen2 = sb("cen2", [P, N])
        sq2 = tn2 = sb("sq2_tn2", [P, N])
        gel = [sb(f"gel{e}", [P, N]) for e in range(2)]
        gated = [sb(f"gated{e}", [P, N]) for e in range(2)]

        q_ps = [ps(f"q_ps{k}", [P, 2, 4 * C]) for k in range(2)]
        b2 = ps("b2", [P, 512])
        b3 = ps("b3", [P, 512])
        b4 = ps("b4", [P, 512])
        b5 = ps("b5", [P, 512])
        b6 = ps("b6", [P, 512])
        b7 = ps("b7", [P, 512])

        xt_in = top["xt_in"]
        xhi_done, xlo_done, rows_zeroed = sem("xhi_done"), sem("xlo_done"), sem("rows_zeroed")
        xr_in = [sem("xr_in0"), sem("xr_in1")]
        qkv_mm, scoresT_mm, scores_mm, av_mm = sem("qkv_mm"), sem("scoresT_mm"), sem("scores_mm"), sem("av_mm")
        z1_mm, cen2_mm, g_mm, var2_mm = sem("z1_mm"), sem("cen2_mm"), sem("g_mm"), sem("var2_mm")
        rstd2_mm, a_mm, out_mm = sem("rstd2_mm"), sem("a_mm"), sem("out_mm")
        raw_out, scoresT_out, z_out, z1_out = sem("raw_out"), sem("scoresT_out"), sem("z_out"), sem("z1_out")
        sq2_out, cen2_out, exp_out, gelu_out = sem("sq2_out"), sem("cen2_out"), sem("exp_out"), sem("gelu_out")
        stats_done, tiny_done, smax_done, shift_done = sem("stats_done"), sem("tiny_done"), sem("smax_done"), sem("shift_done")
        den_done, rden_done, qkv_done, p1_dve = sem("den_done"), sem("rden_done"), sem("qkv_done"), sem("p1_dve")
        p2_dve, tn2_done, gated_done, x_done = sem("p2_dve"), sem("tn2_done"), sem("gated_done"), sem("x_done")
        var2_done = sem("var2_done")
        rstd1_done, rstd2_done, attn_done = sem("rstd1_done"), sem("rstd2_done"), sem("attn_done")
        p1_pool, p2_pool = sem("p1_pool"), sem("p2_pool")

        ident, center = top["consts"][:, K_ID:K_ID + P], top["consts"][:, K_CEN:K_CEN + P]
        cmean = top["consts"][:, K_MEAN:K_MEAN + P]
        cols = top["cols"]
        ND, NP = B - POOL_I, POOL_I
        x_flat = d["x"].rearrange("b c h w -> c b (h w)")
        x_rows = d["x"].rearrange("b c h w -> c b h w")
        xs = top["xs"]

        def upto(n):
            return min(n, TILES) if isinstance(n, int) else n

        def p1_product(eng, k, i, es=slice(0, HD)):
            v = qkv[k]
            n = es.stop - es.start
            q = v[:, i, 0:C].rearrange("p (e h) -> p e h", h=HEADS)[:, es].unsqueeze(2).broadcast_to([P, n, B, HEADS])
            kk = v[:, :, C:2 * C].rearrange("p j (e h) -> p e j h", h=HEADS)[:, es]
            out = prod1[:, es, C * i:C * (i + 1)].rearrange("p e (j h) -> p e j h", h=HEADS)
            return eng.tensor_tensor(out, q, kk, ALU.mult)

        def p2_product(eng, k, j):
            a = attn[:, :].rearrange("p (i j h) -> p j i h", i=B, j=B)[:, j].unsqueeze(3).broadcast_to([P, B, HEADS, HD])
            v = qkv[k][:, j, 2 * C:3 * C].rearrange("p (h e) -> p h e", h=HEADS).unsqueeze(1).broadcast_to([P, B, HEADS, HD])
            out = prod2[:, j, :].rearrange("p (i h e) -> p i h e", i=B, h=HEADS)
            return eng.tensor_tensor(out, a, v, ALU.mult)

        def pe_qkv(pe, t, k, g):
            if g % 2 == 0:
                pe.wait_ge(xlo_done, 2 * t + g // 2 + 1)
            wait(pe, raw_out, 4 * t + g - 1)
            for e in range(2):
                for n, (x, w) in enumerate((("xt_hi", "wcat_hi"), ("xt_hi", "wcat_lo"), ("xt_lo", "wcat_hi"))):
                    m = pe.matmul(q_ps[g % 2][:, e, :], top[x][:, 2 * g + e, :], top[w][:, 2 * g + e, :],
                                  start=(n == 0), stop=(n == 2))
            m.then_inc(qkv_mm, 1)

        def pe_scores_t(pe, t):
            wait(pe, p1_dve, (ND + 1) * (t + 1))
            wait(pe, p1_pool, NP * (t + 1))
            wait(pe, tn2_done, t - 2)
            for blk in range(4):
                for e in range(HD):
                    m = pe.matmul(b2[:, P * blk:P * (blk + 1)], prod1[:, e, P * blk:P * (blk + 1)], ident,
                                  start=(e == 0), stop=(e == HD - 1), is_transpose=True)
            m.then_inc(scoresT_mm, 1)

        def pe_scores(pe, t):
            wait(pe, scoresT_out, t + 1)
            wait(pe, shift_done, t)
            wait(pe, gelu_out, 2 * (t - 1))
            for blk in range(4):
                m = pe.transpose(b3[:, P * blk:P * (blk + 1)], scoresT[:, blk, :], ident)
            m.then_inc(scores_mm, 1)

        def pe_av(pe, t):
            wait(pe, p2_dve, ND * (t + 1))
            wait(pe, p2_pool, NP * (t + 1))
            wait(pe, gated_done, 2 * t - 1)
            for p in range(PAIRS):
                for j in range(B):
                    if p == PAIRS - 1 and j == B - 1:
                        wait(pe, x_done, 4 * (t - 1))
                    m = pe.matmul(b4[:, TILE * p:TILE * (p + 1)], prod2[:, j, P * p:P * (p + 1)], ident,
                                  start=(j == 0), stop=(j == B - 1), is_transpose=True)
            m.then_inc(av_mm, 1)

        def pe_z1(pe, t):
            wait(pe, z_out, t + 1)
            wait(pe, gated_done, 2 * t)
            wait(pe, tkeep_out, t + 1)
            pe.matmul(b6[:, :], top["woutT"][:, :], z[:, :], start=True, stop=False)
            for p in range(PAIRS):
                m = pe.matmul(b6[:, TILE * p:TILE * (p + 1)], tkeep[:, 2 * p:2 * p + 2, :], ident,
                              start=False, stop=(p == PAIRS - 1), is_transpose=True)
            m.then_inc(z1_mm, 1)

        traw = [sb(f"traw{k}", [P, B, C]) for k in range(2)]
        tkeep = sb("tkeep", [P, B, C])
        tkeep_out = sem("tkeep_out")

        def pe_center(pe, t, k):
            wait(pe, z1_out, t + 1)
            pe.matmul(b4[:, :], center, z1[k][:, :], start=True, stop=True).then_inc(cen2_mm, 1)

        def pe_g(pe, t, k, e):
            if e == 1:
                wait(pe, shift_done, upto(t + 2))
            half = slice(C * e, C * e + C)
            pe.matmul((b6, b3)[e][:, :], top["w2T"][half, :], z1[k][half, :], start=True, stop=True).then_inc(g_mm, 1)

        def pe_var2(pe, t):
            wait(pe, sq2_out, t + 1)
            wait(pe, cen2_out, t + 1)
            for p in range(PAIRS):
                m = pe.matmul(b4[:, P * p:P * (p + 1)], sq2[:, TILE * p:TILE * (p + 1)], cmean, start=True, stop=True)
            m.then_inc(var2_mm, 1)

        def pe_rstd2(pe, t):
            wait(pe, rrep_done, t + 1)
            wait(pe, scoresT_out, upto(t + 3))
            for p in range(PAIRS):
                m = pe.transpose(b2[:, TILE * p:TILE * (p + 1)],
                                 rrep[:, 2 * p:2 * p + 2, :].rearrange("p a b -> p (a b)"), ident)
            m.then_inc(rstd2_mm, 1)

        rrep = sb("rrep", [P, B, C])
        rrep_done = sem("rrep_done")

        def pe_a(pe, t, e):
            if e == 0:
                wait(pe, tn2_done, t + 1)
                wait(pe, var2_done, t + 1)
            else:
                wait(pe, gelu_out, 2 * t + 1)
            half = slice(C * e, C * e + C)
            pe.matmul((b4, b6)[e][:, :], top["w1T"][half, :], tn2[half, :], start=True, stop=True).then_inc(a_mm, 1)

        def rows(ap, r):
            return ap.rearrange("p (q r w) -> p r q w", q=PAIRS, r=2)[:, r]

        def out_of(e, r):
            return (b5, b7)[e][C * (1 - r):C * (1 - r) + C, 0:PAIRS * HW]

        def pe_cow(pe, t, k, e):
            if isinstance(t, int):
                wait(pe, x_done, 4 * t)
            half = slice(C * e, C * e + C)
            for r in range(2):
                pe.matmul(out_of(e, r), top["cowT"][half, :], rows(z1[k][half, :], r), start=True, stop=False)

        def pe_out(pe, t, e):
            wait(pe, gated_done, 2 * t + e + 1)
            for r in range(2):
                m = pe.matmul(out_of(e, r), top["w3T"][:, :], rows(gated[e][:, :], r), start=False, stop=True)
            m.then_inc(out_mm, 1)

        def act_xhi(act, t):
            act.wait_ge(xt_in, 16 * (t + 1))
            wait(act, qkv_mm, 4 * t)
            act.activation(top["xt_hi"][0:C, :, :], top["xt"][:, :, :], ACT.Identity).then_inc(xhi_done, 1)

        def pool_xlo(pool, t):
            pool.wait_ge(xhi_done, t + 1)
            wait(pool, xlo_done, 2 * t)
            for half in range(2):
                imgs = slice(half * B // 2, (half + 1) * B // 2)
                pool.tensor_tensor(top["xt_lo"][0:C, imgs, :], top["xt"][:, imgs, :],
                                   top["xt_hi"][0:C, imgs, :].bitcast(F32), ALU.subtract).then_inc(xlo_done, 1)

        def act_raw(act, t, k, g):
            wait(act, qkv_mm, 4 * t + g + 1)
            if g == 0:
                wait(act, tkeep_out, t - 1)
                wait(act, stats_done, B * (t - 1))
                wait(act, qkv_done, B * (t - 1))
            act.activation(traw[k][:, 2 * g:2 * g + 2, :], q_ps[g % 2][:, :, 0:C], ACT.Identity)
            act.activation(raw[k][:, 2 * g:2 * g + 2, :], q_ps[g % 2][:, :, C:4 * C], ACT.Identity)\
                .then_inc(raw_out, 1)

        def act_scores_t(act, t):
            wait(act, scoresT_mm, t + 1)
            wait(act, scores_mm, t)
            act.activation(scoresT[:, :, :].rearrange("p a b -> p (a b)"), b2[:, :], ACT.Identity).then_inc(scoresT_out, 1)

        def act_keep(act, t, k):
            wait(act, raw_out, 4 * (t + 1))
            wait(act, z1_mm, t)
            act.activation(tkeep[:, :, :], traw[k][:, :, :], ACT.Identity).then_inc(tkeep_out, 1)

        def act_z(act, t):
            wait(act, av_mm, t + 1)
            wait(act, z1_mm, t)
            act.activation(z[:, :], b4[:, :], ACT.Identity).then_inc(z_out, 1)

        def act_z1(act, t, k):
            wait(act, z1_mm, t + 1)
            act.activation(z1[k][:, :], b6[:, :], ACT.Identity, bias=cols[:, 1:2]).then_inc(z1_out, 1)

        def act_center(act, t):
            wait(act, cen2_mm, t + 1)
            wait(act, var2_mm, t)
            wait(act, tn2_done, t)
            act.activation(sq2[:, :], b4[:, :], ACT.Square).then_inc(sq2_out, 1)
            act.activation(cen2[:, :], b4[:, :], ACT.Identity).then_inc(cen2_out, 1)

        def act_exp(act, t):
            wait(act, shift_done, t + 1)
            wait(act, attn_done, t)
            wait(act, den_done, t)
            act.activation(exps[:, :], shifted[:, :], ACT.Exp, scale=float(HD) ** -0.5).then_inc(exp_out, 1)

        def act_gelu(act, t, e):
            wait(act, g_mm, 2 * t + e + 1)
            wait(act, gated_done, 2 * t + e - 1)
            act.activation(gel[e][:, :], (b6, b3)[e][:, :], ACT.Gelu, bias=cols[:, 3:4]).then_inc(gelu_out, 1)

        def dve_softmax_max(dve, t):
            wait(dve, scores_mm, t + 1)
            wait(dve, rden_done, t)
            view = b3[:, :].rearrange("p (i j h) -> p i h j", i=B, j=B)
            dve.tensor_reduce(smax[:, :].rearrange("p (i h) -> p i h", i=B), view, AX.X, ALU.max).then_inc(smax_done, 1)
            wait(dve, smax_done, t + 1)
            wait(dve, attn_done, t)
            top_of = smax[:, :].rearrange("p (i h) -> p i h", i=B).unsqueeze(2).broadcast_to([P, B, B, HEADS])
            dve.tensor_tensor(shifted[:, :].rearrange("p (i j h) -> p i j h", i=B, j=B),
                              b3[:, :].rearrange("p (i j h) -> p i j h", i=B, j=B), top_of, ALU.subtract)\
                .then_inc(shift_done, 1)

        def dve_softmax_sum(dve, t):
            wait(dve, exp_out, t + 1)
            wait(dve, rden_done, t)
            dve.tensor_reduce(den[:, :].rearrange("p (i h) -> p i h", i=B),
                              exps[:, :].rearrange("p (i j h) -> p i h j", i=B, j=B), AX.X, ALU.add).then_inc(den_done, 1)
            wait(dve, den_done, t + 1)
            wait(dve, attn_done, t)
            dve.reciprocal(rden[:, :], den[:, :]).then_inc(rden_done, 1)

        def dve_stats(dve, t, k, g):
            wait(dve, raw_out, 4 * t + g + 1)
            if g == 0:
                wait(dve, tiny_done, 5 * t)
            for i in (2 * g, 2 * g + 1):
                dve.bn_stats(st1[:, i, :], traw[k][:, i, :]).then_inc(stats_done, 1)

        def dve_var1(dve, t, step):
            if step == 0:
                wait(dve, stats_done, B * (t + 1))
                wait(dve, rstd1_done, t)
                dve.tensor_tensor(tiny[:, 0, :], st1[:, :, 1], st1[:, :, 4], ALU.subtract).then_inc(tiny_done, 1)
                dve.tensor_tensor(tiny[:, 1, :], st1[:, :, 2], st1[:, :, 5], ALU.add).then_inc(tiny_done, 1)
            if step == 1:
                wait(dve, tiny_done, 5 * t + 2)
                dve.scalar_tensor_tensor(tiny[:, 2, :], tiny[:, 0, :], 0.25, tiny[:, 0, :], ALU.mult, ALU.mult)\
                    .then_inc(tiny_done, 1)
                dve.tensor_scalar(tiny[:, 1, :], tiny[:, 1, :], 1.0 / C, 1e-5, ALU.mult, ALU.add).then_inc(tiny_done, 1)
            if step == 2:
                wait(dve, tiny_done, 5 * t + 4)
                dve.tensor_tensor(tiny[:, 3, :], tiny[:, 2, :], tiny[:, 1, :], ALU.add).then_inc(tiny_done, 1)

        def dve_qkv(dve, t, k):
            wait(dve, rstd1_done, t + 1)
            wait(dve, p2_pool, NP * (t - 1))
            wait(dve, p2_dve, ND * (t - 1))
            for i in range(B):
                dve.scalar_tensor_tensor(qkv[k][:, i, :], raw[k][:, i, :], rstd1[:, i:i + 1], top["brep"][:, :],
                                         ALU.mult, ALU.add).then_inc(qkv_done, 1)

        def dve_p1(dve, t, k, images):
            wait(dve, qkv_done, B * (t + 1))
            wait(dve, scoresT_mm, t)
            for i in images:
                p1_product(dve, k, i).then_inc(p1_dve, 1)
            p1_product(dve, k, ND, slice(0, HD // 2)).then_inc(p1_dve, 1)

        def dve_rrep(dve, t):
            wait(dve, rstd2_done, t + 1)
            wait(dve, rstd2_mm, t)
            dve.tensor_scalar(rrep[:, :, :], rstd2[:, :].unsqueeze(2).broadcast_to([P, B, C]), 1.0, None, ALU.mult)\
                .then_inc(rrep_done, 1)

        def dve_p2(dve, t, k, js):
            wait(dve, attn_done, t + 1)
            wait(dve, av_mm, t)
            for j in js:
                p2_product(dve, k, j).then_inc(p2_dve, 1)

        def dve_var2(dve, t):
            wait(dve, var2_mm, t + 1)
            wait(dve, rstd2_done, t)
            dve.tensor_scalar(var2[:, :], b4[:, ::C], 1e-5, None, ALU.add).then_inc(var2_done, 1)

        def dve_tn2(dve, t):
            wait(dve, rstd2_mm, t + 1)
            wait(dve, cen2_out, t + 1)
            wait(dve, a_mm, 2 * t)
            dve.tensor_tensor(tn2[:, :], b2[:, :], cen2[:, :], ALU.mult).then_inc(tn2_done, 1)

        def dve_gated(dve, t, e):
            wait(dve, a_mm, 2 * t + e + 1)
            wait(dve, gelu_out, 2 * t + e + 1)
            wait(dve, out_mm, 2 * t + e - 1)
            dve.scalar_tensor_tensor(gated[e][:, :], (b4, b6)[e][:, :], cols[:, 2:3], gel[e][:, :], ALU.add, ALU.mult)\
                .then_inc(gated_done, 1)

        def dve_x(dve, t, k, e, rs=(0, 1)):
            if isinstance(t, int):
                dve.wait_ge(xr_in[k], 32 * ((t - k) // 2 + 1))
            else:
                dve.wait_ge(xr_in[k], (t - k) * 16 + 32)
            wait(dve, out_mm, 2 * t + e + 1)
            for r in rs:
                half = slice(C * (1 - r), C * (1 - r) + C)
                dve.scalar_tensor_tensor(
                    xs[half, e::2, bass.ds(t + r, 1), :].rearrange("p q s w -> p q (s w)"),
                    out_of(e, r).rearrange("p (q w) -> p q w", q=PAIRS), cols[half, 4:5], xr[k][half, e::2, :],
                    ALU.add, ALU.add).then_inc(x_done, 1)

        def pool_rstd1(pool, t):
            wait(pool, tiny_done, 5 * t + 5)
            wait(pool, qkv_done, B * t)
            pool.tensor_tensor(rstd1[:, :], tiny[:, 3, :], top["half"][:, :], ALU.pow).then_inc(rstd1_done, 1)

        def pool_attn(pool, t):
            wait(pool, rden_done, t + 1)
            wait(pool, p2_dve, ND * t)
            wait(pool, p2_pool, NP * t)
            r = rden[:, :].rearrange("p (i h) -> p i h", i=B).unsqueeze(2).broadcast_to([P, B, B, HEADS])
            pool.tensor_tensor(attn[:, :].rearrange("p (i j h) -> p i j h", i=B, j=B),
                               exps[:, :].rearrange("p (i j h) -> p i j h", i=B, j=B), r, ALU.mult).then_inc(attn_done, 1)

        def pool_p2(pool, t, k, js):
            wait(pool, attn_done, t + 1)
            wait(pool, av_mm, t)
            for j in js:
                p2_product(pool, k, j).then_inc(p2_pool, 1)

        def pool_rstd2(pool, t):
            wait(pool, var2_done, t + 1)
            wait(pool, rrep_done, t)
            pool.tensor_tensor(rstd2[:, :], var2[:, :], top["half"][:, :], ALU.pow).then_inc(rstd2_done, 1)

        def pool_p1(pool, t, k):
            wait(pool, qkv_done, B * (t + 1))
            wait(pool, scoresT_mm, t)
            for i in range(ND, B):
                p1_product(pool, k, i, slice(HD // 2 if i == ND else 0, HD)).then_inc(p1_pool, 1)

        def sp_xt(sp, t):
            wait(sp, xlo_done, 2 * t)
            src = x_flat[:, :, bass.ds(t * TILE, TILE)]
            sp.dma_start(top["xt"][:, :, :], src).then_inc(xt_in, 16)

        def sp_xr(sp, t, k):
            wait(sp, x_done, 4 * (t - 1))
            for r in range(2):
                half = slice(C * (1 - r), C * (1 - r) + C)
                sp.dma_start(xr[k][half, :, :],
                             x_rows[:, :, bass.ds(2 * t + r, 1), :].rearrange("c b r w -> c b (r w)")).then_inc(xr_in[k], 16)

        def pe_iteration(pe, t, k, new, mid, cur, old, last):
            if mid:
                pe_scores_t(pe, t + 1)
            if new:
                pe_qkv(pe, t + 2, k, 0)
            if old:
                pe_rstd2(pe, t - 1)
            if mid:
                pe_scores(pe, t + 1)
            if new:
                pe_qkv(pe, t + 2, k, 1)
                pe_qkv(pe, t + 2, k, 2)
            if old:
                pe_a(pe, t - 1, 0)
                pe_a(pe, t - 1, 1)
            if new:
                pe_qkv(pe, t + 2, k, 3)
            if cur:
                pe_av(pe, t)
            if old:
                pe_cow(pe, t - 1, 1 - k, 0)
                pe_cow(pe, t - 1, 1 - k, 1)
            if cur:
                pe_z1(pe, t)
            if old:
                pe_out(pe, t - 1, 0)
                pe_out(pe, t - 1, 1)
            if cur:
                pe_center(pe, t, k)
                pe_g(pe, t, k, 0)
                pe_g(pe, t, k, 1)
                pe_var2(pe, t)

        def act_iteration(act, t, k, new, mid, cur, old, last):
            if cur:
                act_keep(act, t, k)
            if mid:
                act_scores_t(act, t + 1)
            if new:
                act_raw(act, t + 2, k, 0)
                act_raw(act, t + 2, k, 1)
            if mid:
                act_exp(act, t + 1)
            if new:
                act_raw(act, t + 2, k, 2)
                act_raw(act, t + 2, k, 3)
            if not isinstance(t, int) or t + 3 < TILES:
                act_xhi(act, t + 3)
            if cur:
                act_z(act, t)
                act_z1(act, t, k)
                act_center(act, t)
                act_gelu(act, t, 0)
                act_gelu(act, t, 1)

        def dve_iteration(dve, t, k, new, mid, cur, old, last):
            if cur:
                dve_p2(dve, t, k, range(0, 2))
            if old:
                dve_rrep(dve, t - 1)
            if cur:
                dve_p2(dve, t, k, range(2, ND))
            if old:
                dve_tn2(dve, t - 1)
            if mid:
                dve_softmax_max(dve, t + 1)
            if new:
                dve_stats(dve, t + 2, k, 0)
                dve_stats(dve, t + 2, k, 1)
            if old:
                dve_gated(dve, t - 1, 0)
                dve_gated(dve, t - 1, 1)
            if last:
                dve_x(dve, t - 2, k, 0, (0,))
            if new:
                dve_stats(dve, t + 2, k, 2)
                dve_stats(dve, t + 2, k, 3)
            for step in range(3):
                if new:
                    dve_var1(dve, t + 2, step)
                if last:
                    dve_x(dve, t - 2, k, *((0, (1,)), (1, (0,)), (1, (1,)))[step])
            if mid:
                dve_softmax_sum(dve, t + 1)
            if new:
                dve_qkv(dve, t + 2, k)
                dve_p1(dve, t + 2, k, range(ND))
            if cur:
                dve_var2(dve, t)

        def pool_iteration(pool, t, k, new, mid, cur, old, last):
            if old:
                pool_rstd2(pool, t - 1)
            if new:
                pool_xlo(pool, t + 2)
            if cur:
                pool_p2(pool, t, k, range(ND, B))
            if new:
                pool_rstd1(pool, t + 2)
            if mid:
                pool_attn(pool, t + 1)
            if new:
                pool_p1(pool, t + 2, k)

        def sp_iteration(sp, t, k, new, mid, cur, old, last):
            if not isinstance(t, int) or t + 4 < TILES:
                sp_xt(sp, t + 4)
            if cur:
                sp_xr(sp, t, k)

        def run(eng, iteration):
            def peeled(t):
                exists = [0 <= u < TILES for u in (t + 2, t + 1, t, t - 1, t - 2)]
                iteration(eng, t, t % 2, *exists)

            first, last = 4, TILES - 4
            for t in range(-2, first):
                peeled(t)
            with eng.Fori(first // 2, last // 2) as pair:
                for k in range(2):
                    iteration(eng, pair * 2 + k, k, True, True, True, True, True)
            for t in range(last, TILES + 2):
                peeled(t)

        block = ctx.enter_context(nc.Block())

        @block.tensor
        def _(pe):
            run(pe, pe_iteration)

        @block.scalar
        def _(act):
            act_xhi(act, 0)
            run(act, act_iteration)

        @block.vector
        def _(dve):
            dve.memset(xs[0:C, :, 0, :], 0.0).then_inc(rows_zeroed, 1)
            dve.memset(xs[C:P, :, SLOTS - 1, :], 0.0).then_inc(rows_zeroed, 1)
            run(dve, dve_iteration)

        @block.gpsimd
        def _(pool):
            run(pool, pool_iteration)

        @block.sync
        def _(sp):
            sp_xt(sp, 1)
            run(sp, sp_iteration)


def conv_steps(nc, d, top):
    with ExitStack() as ctx:
        def sb(name, shape, dt=F32):
            return ctx.enter_context(nc.sbuf_tensor(name, shape, dt))

        def sem(name):
            return ctx.enter_context(nc.semaphore(name))

        QA = [(0, 7), (7, 7), (14, 7), (21, 6), (27, 6)]
        QM = [(8 * q, 8) for q in range(4)]
        NA, NM = len(QA), len(QM)
        PER_STEP = NA + NM
        PER_IMAGE = STEPS * PER_STEP
        MOST = 8
        RING = 3
        tiles = [(s, c, q) for s in range(STEPS) for c in range(2) for q in range((NM, NA)[c])]

        xs, cols = top["xs"], top["cols"]
        a_hi, a_lo = (sb(n, [P, SLOTS, PRODS, DUO], F32R) for n in ("a_hi", "a_lo"))
        m_hi, m_lo = (sb(n, [P, SLOTS + 1, PRODS, DUO], F32R) for n in ("m_hi", "m_lo"))
        m1b = [sb(f"m1b{k}", [P, MOST, DUO]) for k in range(RING)]
        duo = [sb(f"duo{k}", [P, 2, MOST, DUO]) for k in range(RING)]
        hidden = [sb(f"hidden{k}", [P, MOST, PADW]) for k in range(RING)]
        mixed = [sb(f"mixed{k}", [P, MOST, PRODS, DUO]) for k in range(RING)]
        cur = sb("cur", [P, SLOTS, PADW])
        banks = [[ctx.enter_context(nc.psum_tensor(f"conv{k}_{h}", [P, 2, MOST, DUO], F32)) for h in range(2)]
                 for k in range(4)]
        zeroed, conv_mm, m1_out, sums_done, duo_done = sem("zeroed"), sem("conv_mm"), sem("m1_out"), sem("sums_done"), sem("duo_done")
        relu_done, x_added, mix03_done, mix12_done = sem("relu_done"), sem("x_added"), sem("mix03_done"), sem("mix12_done")
        hi03_done, hi12_done, lo03_done, lo12_done = sem("hi03_done"), sem("hi12_done"), sem("lo03_done"), sem("lo12_done")
        result_done, stored = sem("result_done"), sem("stored")
        fetched, staged = sem("fetched"), sem("staged")
        ZEROED = 1 + 4 + RING

        def slot_tile(slots, last):
            return [q for q, (s0, cnt) in enumerate(slots) if s0 <= last < s0 + cnt][0]

        def bank_free(n):
            before = [k for k in range(n) if k % 4 == n % 4]
            return before[-1] + 1 if before else [k for k in range(PER_IMAGE) if k % 4 == n % 4][-1] + 1 - PER_IMAGE

        def pairs(view):
            return view.rearrange("p s (j two) -> p two s j", two=2)

        def stored_tile(img, s0, cnt):
            return xs[:, bass.ds(img, 1), s0:s0 + cnt, :].rearrange("p b s w -> p (b s) w")

        def fetch(act, q, x):
            s0, cnt = QA[q]
            act.activation(cur[:, s0:s0 + cnt, 1:1 + HW], x, ACT.Identity).then_inc(fetched, 1)

        def target(n):
            s, c, q = tiles[n]
            s0, cnt = (QM, QA)[c][q]
            hi, lo = ((m_hi, m_lo), (a_hi, a_lo))[c]
            s0 += 1 - c
            return hi[:, s0:s0 + cnt, :, :], lo[:, s0:s0 + cnt, :, :], cnt

        def mixes(last, n):
            return not (last and n >= PER_IMAGE - NA)

        def mix03(eng, src, cnt, v, r):
            if not (isinstance(v, int) and v < RING):
                eng.wait_ge(lo03_done, v - RING + 1)
            eng.tensor_tensor(mixed[r][:, 0:cnt, 0:2, :].rearrange("p s two j -> p two s j"),
                              pairs(src[:, :, 0:HW]), pairs(src[:, :, 2:2 + HW]), ALU.subtract).then_inc(mix03_done, 1)

        def mix12(eng, src, cnt, v, r):
            if not (isinstance(v, int) and v < RING):
                eng.wait_ge(lo12_done, v - RING + 1)
            even = src[:, :, 1:1 + HW].rearrange("p s (j two) -> p s j two", two=2)[:, :, :, 0]
            odd = src[:, :, 1:1 + HW].rearrange("p s (j two) -> p s j two", two=2)[:, :, :, 1]
            eng.tensor_tensor(mixed[r][:, 0:cnt, 2, :], even, odd, ALU.add).then_inc(mix12_done, 1)
            eng.tensor_tensor(mixed[r][:, 0:cnt, 3, :], odd, even, ALU.subtract).then_inc(mix12_done, 1)

        def act_hi03(act, exists, n, v, r):
            if exists:
                hi, lo, cnt = target(n)
                act.wait_ge(mix03_done, v + 1)
                act.activation(hi[:, :, 0:2, :], mixed[r][:, 0:cnt, 0:2, :], ACT.Identity).then_inc(hi03_done, 1)

        def act_hi12(act, exists, n, v, r):
            if exists:
                hi, lo, cnt = target(n)
                act.wait_ge(mix12_done, 2 * v + 2)
                act.activation(hi[:, :, 2:4, :], mixed[r][:, 0:cnt, 2:4, :], ACT.Identity).then_inc(hi12_done, 1)

        def dve_lo(dve, n, v, r):
            hi, lo, cnt = target(n)
            dve.wait_ge(hi03_done, v + 1)
            dve.tensor_tensor(lo[:, :, 0:2, :], mixed[r][:, 0:cnt, 0:2, :], hi[:, :, 0:2, :].bitcast(F32),
                              ALU.subtract).then_inc(lo03_done, 1)

        def pool_lo(pool, n, v, r):
            hi, lo, cnt = target(n)
            pool.wait_ge(hi12_done, v + 1)
            pool.tensor_tensor(lo[:, :, 2:4, :], mixed[r][:, 0:cnt, 2:4, :], hi[:, :, 2:4, :].bitcast(F32),
                               ALU.subtract).then_inc(lo12_done, 1)

        def pe_image(pe, img, first):
            base = img * PER_IMAGE
            for n, (s, c, q) in enumerate(tiles):
                need = bank_free(n)
                if not (first and need <= 0):
                    pe.wait_ge(duo_done, base + need)
                s0, cnt = (QM, QA)[c][q]
                if c == 0:
                    v = s * PER_STEP + slot_tile(QA, s0 + cnt)
                else:
                    v = s * PER_STEP + NA + slot_tile(QM, min(s0 + cnt - 1, SLOTS - 2))
                pe.wait_ge(lo03_done, base + v + 1)
                pe.wait_ge(lo12_done, base + v + 1)
                hi, lo = ((a_hi, a_lo), (m_hi, m_lo))[c]
                wh, wl = top["cwh"][c], top["cwl"][c]
                for j in range(PRODS):
                    k = 0
                    for slot in range(2):
                        for w, x in ((wh, hi), (wh, lo), (wl, hi)):
                            m = pe.matmul(banks[n % 4][j // 2][:, j % 2, 0:cnt, :], w[:, slot, j, :],
                                          x[:, s0 + slot:s0 + slot + cnt, j, :], start=(k == 0), stop=(k == 5))
                            k += 1
                m.then_inc(conv_mm, 1)

        def act_m1(act, img, n, first):
            s, c, q = tiles[n]
            cnt = (QM, QA)[c][q][1]
            act.wait_ge(conv_mm, img * PER_IMAGE + n + 1)
            if not (first and n < RING):
                act.wait_ge(sums_done, 2 * (img * PER_IMAGE + n - RING + 1))
            act.activation(m1b[n % RING][:, 0:cnt, :], banks[n % 4][1][:, 0, 0:cnt, :], ACT.Identity,
                           bias=cols[:, (6, 8)[c]:(7, 9)[c]]).then_inc(m1_out, 1)

        def act_result(act, img, n, last):
            s, c, q = tiles[n]
            s0, cnt = QA[q]
            act.wait_ge(x_added, img * (XA * STEPS) + XA * s + adds(q + 1))
            act.activation(stored_tile(img, s0, cnt), cur[:, s0:s0 + cnt, 1:1 + HW], ACT.Relu).then_inc(result_done, 1)
            if not last:
                act.wait_ge(staged, img * NA + q + 1)
                act.wait_ge(result_done, img * NA + q + 1)
                fetch(act, q, hidden[n % RING][:, 0:cnt, 1:1 + HW])

        def act_image(act, img, first, last):
            base = img * PER_IMAGE
            for n, (s, c, q) in enumerate(tiles):
                s0, cnt = (QM, QA)[c][q]
                act_m1(act, img, n, first)
                if c == 1 and s == STEPS - 1 and not last:
                    act.activation(hidden[n % RING][:, 0:cnt, 1:1 + HW], stored_tile(img + 1, s0, cnt), ACT.Identity)\
                        .then_inc(staged, 1)
                act_hi12(act, mixes(last, n - 2), n - 2, base + n - 2 + NA, (n - 2 + NA) % RING)
                act_hi03(act, mixes(last, n - 1), n - 1, base + n - 1 + NA, (n - 1 + NA) % RING)
                if c == 0:
                    act.wait_ge(duo_done, base + n + 1)
                    act.activation(pairs(hidden[n % RING][:, 0:cnt, 1:1 + HW]), duo[n % RING][:, :, 0:cnt, :], ACT.Relu)\
                        .then_inc(relu_done, 1)
                elif s == STEPS - 1:
                    if q > 0:
                        act_result(act, img, n - 1, last)
                    if q == NA - 1:
                        act_result(act, img, n, last)

        XA = NA + 2

        def adds(q):
            return q + (q >= 1) + (q == NA)

        def dve_image(dve, img, first, last):
            base = img * PER_IMAGE
            for n, (s, c, q) in enumerate(tiles):
                s0, cnt = (QM, QA)[c][q]
                y = duo[n % RING]
                dve.wait_ge(m1_out, base + n + 1)
                for half, op in ((0, ALU.add), (1, ALU.subtract)):
                    dve.tensor_tensor(y[:, half, 0:cnt, :], m1b[n % RING][:, 0:cnt, :], banks[n % 4][1][:, 1, 0:cnt, :],
                                      op).then_inc(sums_done, 1)
                dve.wait_ge(sums_done, 2 * (base + n + 1))
                dve.tensor_tensor(y[:, :, 0:cnt, :], y[:, :, 0:cnt, :], banks[n % 4][0][:, :, 0:cnt, :], ALU.add)\
                    .then_inc(duo_done, 1)
                if mixes(last, n - 1):
                    dve_lo(dve, n - 1, base + n - 1 + NA, (n - 1 + NA) % RING)
                if c == 1:
                    dve.wait_ge(duo_done, base + n + 1)
                    if s == 0:
                        dve.wait_ge(fetched, img * NA + q + 1)
                    parts = [(slice(0, P), s0, cnt)]
                    if q == 0:
                        parts = [(slice(C, P), 0, 1), (slice(0, P), 1, cnt - 1)]
                    if q == NA - 1:
                        parts = [(slice(0, P), s0, cnt - 1), (slice(0, C), SLOTS - 1, 1)]
                    for part, p0, pc in parts:
                        xv = pairs(cur[part, p0:p0 + pc, 1:1 + HW])
                        dve.tensor_tensor(xv, xv, y[part, :, p0 - s0:p0 - s0 + pc, :], ALU.add).then_inc(x_added, 1)
                if mixes(last, n):
                    mix03(dve, source(dve, img, n), cnt, base + n + NA, (n + NA) % RING)

        def source(eng, img, n):
            s, c, q = tiles[n]
            s0, cnt = (QM, QA)[c][q]
            if c == 0:
                eng.wait_ge(relu_done, img * (NM * STEPS) + NM * s + q + 1)
                return hidden[n % RING][:, 0:cnt, :]
            if s < STEPS - 1:
                eng.wait_ge(x_added, img * (XA * STEPS) + XA * s + adds(q + 1))
            else:
                eng.wait_ge(staged, img * NA + q + 1)
                return hidden[n % RING][:, 0:cnt, :]
            return cur[:, s0:s0 + cnt, :]

        def pool_image(pool, img, first, last):
            base = img * PER_IMAGE
            for n, (s, c, q) in enumerate(tiles):
                if mixes(last, n - 2):
                    pool_lo(pool, n - 2, base + n - 2 + NA, (n - 2 + NA) % RING)
                if mixes(last, n):
                    cnt = (QM, QA)[c][q][1]
                    mix12(pool, source(pool, img, n), cnt, base + n + NA, (n + NA) % RING)

        def first_mix(eng, mix, split, lag):
            for q, (s0, cnt) in enumerate(QA):
                eng.wait_ge(fetched, q + 1)
                mix(eng, cur[:, s0:s0 + cnt, :], cnt, q, q % RING)
                if q < NA - lag:
                    split(eng, PER_IMAGE - NA + q, q, q % RING)

        out = d["out"].rearrange("b c (p r) w -> b r c p w", r=2)
        STORED = 16 * 2 * NM

        def sp_image(sp, img):
            for q in range(NM):
                s0 = 8 * q
                sp.wait_ge(result_done, img * NA + slot_tile(QA, s0 + 8) + 1)
                sp.dma_start(out[bass.ds(img, 1), 0, :, s0:s0 + 8, :].rearrange("b c p w -> (b c) p w"),
                             xs[C:P, bass.ds(img, 1), s0:s0 + 8, :].rearrange("c b p w -> c (b p) w")).then_inc(stored, 16)
                sp.dma_start(out[bass.ds(img, 1), 1, :, s0:s0 + 8, :].rearrange("b c p w -> (b c) p w"),
                             xs[0:C, bass.ds(img, 1), s0 + 1:s0 + 9, :].rearrange("c b p w -> c (b p) w")).then_inc(stored, 16)

        block = ctx.enter_context(nc.Block())

        @block.tensor
        def _(pe):
            pe.wait_ge(zeroed, ZEROED)
            pe_image(pe, 0, True)
            with pe.Fori(1, B) as img:
                pe_image(pe, img, False)

        @block.scalar
        def _(act):
            act.wait_ge(zeroed, ZEROED)
            for q in range(2):
                fetch(act, q, stored_tile(0, *QA[q]))
            for q in range(NA - 1):
                if q + 2 < NA:
                    fetch(act, q + 2, stored_tile(0, *QA[q + 2]))
                act_hi03(act, True, PER_IMAGE - NA + q, q, q % RING)
                if q < NA - 2:
                    act_hi12(act, True, PER_IMAGE - NA + q, q, q % RING)
            act_image(act, 0, True, False)
            with act.Fori(1, B - 1) as img:
                act_image(act, img, False, False)
            act_image(act, B - 1, False, True)

        @block.vector
        def _(dve):
            dve.memset(cur[:, :, 0:PADW:PADW - 1], 0.0).then_inc(zeroed, 1)
            for t in (m_hi, m_lo):
                dve.memset(t[:, 0, :, :].bitcast(F32), 0.0).then_inc(zeroed, 1)
                dve.memset(t[:, SLOTS, :, :].bitcast(F32), 0.0).then_inc(zeroed, 1)
            for t in hidden:
                dve.memset(t[:, :, 0:PADW:PADW - 1], 0.0).then_inc(zeroed, 1)
            dve.wait_ge(zeroed, ZEROED)
            first_mix(dve, mix03, dve_lo, 1)
            dve_image(dve, 0, True, False)
            with dve.Fori(1, B - 1) as img:
                dve_image(dve, img, False, False)
            dve_image(dve, B - 1, False, True)

        @block.gpsimd
        def _(pool):
            pool.wait_ge(zeroed, ZEROED)
            first_mix(pool, mix12, pool_lo, 2)
            pool_image(pool, 0, True, False)
            with pool.Fori(1, B - 1) as img:
                pool_image(pool, img, False, False)
            pool_image(pool, B - 1, False, True)

        @block.sync
        def _(sp):
            with sp.Fori(0, B) as img:
                sp_image(sp, img)
            sp.wait_ge(stored, STORED * B)


def program(nc, d):
    with ExitStack() as ctx:
        def sb(name, shape, dt=F32):
            return ctx.enter_context(nc.sbuf_tensor(name, shape, dt))

        top = {
            "cols": sb("cols", [P, 9]),
            "cwh": [sb(f"cwh{k}", [P, 2, PRODS, P], F32R) for k in range(2)],
            "cwl": [sb(f"cwl{k}", [P, 2, PRODS, P], F32R) for k in range(2)],
            "xs": sb("xs", [P, B, SLOTS, HW]),
        }
        top["xt_in"] = ctx.enter_context(nc.semaphore("xt_in"))
        with ExitStack() as inner:
            def sbi(name, shape, dt=F32):
                return inner.enter_context(nc.sbuf_tensor(name, shape, dt))

            top.update({
                "consts": sbi("consts", [P, K_GRP]),
                "half": sbi("half", [P, B]),
                "xt": sbi("xt", [C, B, TILE]),
                "xt_hi": sbi("xt_hi", [C + 1, B, TILE], F32R), "xt_lo": sbi("xt_lo", [C + 1, B, TILE], F32R),
                "wcat_hi": sbi("wcat_hi", [C + 1, B, 4 * C], F32R), "wcat_lo": sbi("wcat_lo", [C + 1, B, 4 * C], F32R),
                "woutT": sbi("woutT", [P, P]), "cowT": sbi("cowT", [P, C]),
                "w1T": sbi("w1T", [P, HID]), "w2T": sbi("w2T", [P, HID]), "w3T": sbi("w3T", [HID, C]),
                "brep": sbi("brep", [P, 3 * C]),
            })
            setup_weights(nc, d, top)
            attention_block(nc, d, top)
        conv_steps(nc, d, top)


_INS = ["x"] + ["L0_conv_" + n for n in (
    "gn_g gn_b ciw cib pe ln1g ln1b wq bq wk bk wv bv win bin_ wout bout ln2g ln2b w1 b1 w2 b2 w3 b3 cow cob").split()] \
    + ["L1_conv_" + n for n in "w1 b1 w2 b2".split()]


def kernel(**inputs):
    import numpy as np
    import concourse.bacc as bacc
    from concourse import mybir as mb
    from concourse.bass_utils import run_bass_kernel_spmd

    consts = np.zeros((P, K_END), np.float32)
    consts[:, K_ID:K_ID + P] = np.eye(P)
    for k in range(2):
        half = slice(C * k, C * k + C)
        consts[half, K_CEN + C * k:K_CEN + C * k + C] = np.eye(C) - 1.0 / C
        consts[half, K_MEAN + C * k:K_MEAN + C * k + C] = 1.0 / C
    for g in range(P // 8):
        consts[8 * g:8 * g + 8, K_GRP + 8 * g:K_GRP + 8 * g + 8] = 1.0 / 8

    nc = bacc.Bacc("TRN2", target_bir_lowering=False, num_devices=1)
    arrays, d = {}, {}
    for name in _INS:
        a = np.ascontiguousarray(inputs[name])
        arrays[f"in_{name}"] = a
        d[name] = nc.dram_tensor(f"in_{name}", a.shape, mb.dt.from_np(a.dtype), kind="ExternalInput").ap()
    arrays["in_consts"] = consts
    d["consts"] = nc.dram_tensor("in_consts", consts.shape, mb.dt.float32, kind="ExternalInput").ap()
    d["out"] = nc.dram_tensor("out_y", (B, C, HW, HW), mb.dt.float32, kind="ExternalOutput").ap()
    program(nc, d)
    r = run_bass_kernel_spmd(nc, [arrays], core_ids=[0])
    return r.results[0]["out_y"]
```
